# Optimizing a Trainium2 kernel written in Bass

```python
import numpy as np
import jax
import jax.numpy as jnp

def _softmax(x, axis=-1):
    return jax.nn.softmax(x, axis=axis)

def _gelu(x):
    return jax.nn.gelu(x, approximate=True)

def _silu(x):
    return jax.nn.silu(x)

def _sigmoid(x):
    return jax.nn.sigmoid(x)

def _layernorm(x, axis=-1, eps=1e-05):
    m = jnp.mean(x, axis=axis, keepdims=True)
    v = jnp.var(x, axis=axis, keepdims=True)
    return (x - m) / jnp.sqrt(v + eps)

def _scatter_add(tgt, idx, src, axis=0):
    return tgt.at[idx].add(src)

def _segment_sum(src, seg, n):
    return jax.ops.segment_sum(src, seg, n)
kernel_name = 'mk_gnn_preln_d2_gnn_r8_a70aa5'

def setup_inputs(seed: int=0):
    np.random.seed(seed)
    _w = jnp.asarray

    def _rec_inputs():
        import jax
        import jax.numpy as jnp
        _gk = jax.random.key(seed)
        x = -0.0005121 + 1.001 * jax.random.normal(jax.random.fold_in(_gk, 1), (12500, 32), jnp.float32)
        src = jax.random.randint(jax.random.fold_in(_gk, 2), (200000,), 0, 12500, jnp.int32)
        dst = jnp.minimum((12500 * jax.random.uniform(jax.random.fold_in(_gk, 3), (200000,)) ** 2.0).astype(jnp.int32), 99999)
        _o = jnp.argsort(dst, stable=True)
        src = src[_o]
        dst = dst[_o]
        edge_attr_4 = 0.000398945 + 1.00003 * jax.random.normal(jax.random.fold_in(_gk, 12), (200000, 4), jnp.float32)
        node_vec1 = jax.random.uniform(jax.random.fold_in(_gk, 14), (12500, 1), jnp.float32, 0.0, 0.999991)
        node_vec1_n2 = jax.random.uniform(jax.random.fold_in(_gk, 15), (12500, 1), jnp.float32, 0.0, 0.999991)
        return (x, src, dst, edge_attr_4, node_vec1, node_vec1_n2)
    x, src, dst, edge_attr_4, node_vec1, node_vec1_n2 = _rec_inputs()

    def _L0_gnn_setup():
        import jax, jax.numpy as jnp
        import numpy as np
        N_NODES = 12500
        N_EDGES = 200000
        D_FEAT = 32
        key = jax.random.key(seed)
        k1, k2, k3, k4, k5 = jax.random.split(key, 5)
        src_feats = jax.random.normal(k1, (N_NODES, D_FEAT), dtype=jnp.float32)
        cj = jax.random.uniform(k2, (N_NODES, 1), dtype=jnp.float32)
        ci = jax.random.uniform(k3, (N_NODES, 1), dtype=jnp.float32)
        src_idx = jax.random.randint(k4, (N_EDGES,), 0, N_NODES, dtype=jnp.int32)
        dst_idx = jax.random.randint(k5, (N_EDGES,), 0, N_NODES, dtype=jnp.int32)
        return {'src_feats': src_feats, 'cj': cj, 'ci': ci, 'src_idx': src_idx, 'dst_idx': dst_idx}
    _L0_gnn_all = _L0_gnn_setup()
    _L0_gnn_in = {k: v for k, v in _L0_gnn_all.items() if k in ()}
    del _L0_gnn_all

    def _L1_gnn_setup():
        import jax, jax.numpy as jnp
        import numpy as np
        N_NODES = 12500
        N_EDGES = 200000
        IN_DIM = 32
        HID = 64
        OUT_DIM = 32
        EDGE_DIM = 4
        key = jax.random.key(seed)
        ks = jax.random.split(key, 12)
        x = jax.random.normal(ks[0], (N_NODES, IN_DIM), dtype=jnp.float32)
        edge_index = jax.random.randint(ks[1], (2, N_EDGES), 0, N_NODES, dtype=jnp.int32)
        edge_attr = jax.random.normal(ks[2], (N_EDGES, EDGE_DIM), dtype=jnp.float32)

        def lin(k, fan_in, fan_out):
            kw, kb = jax.random.split(k)
            bound = 1.0 / np.sqrt(fan_in)
            W = jax.random.uniform(kw, (fan_in, fan_out), minval=-bound, maxval=bound, dtype=jnp.float32)
            b = jax.random.uniform(kb, (fan_out,), minval=-bound, maxval=bound, dtype=jnp.float32)
            return (W, b)
        W1, b1 = lin(ks[3], 2 * IN_DIM, HID)
        W2, b2 = lin(ks[4], HID, 2 * HID)
        W3, b3 = lin(ks[5], 2 * HID, HID)
        W4, b4 = lin(ks[6], HID, OUT_DIM)
        return {'x': x, 'edge_index': edge_index, 'edge_attr': edge_attr, 'W1': W1, 'b1': b1, 'W2': W2, 'b2': b2, 'W3': W3, 'b3': b3, 'W4': W4, 'b4': b4}
    _L1_gnn_all = _L1_gnn_setup()
    _L1_gnn_in = {k: v for k, v in _L1_gnn_all.items() if k in ('W1', 'b1', 'W2', 'b2', 'W3', 'b3', 'W4', 'b4')}
    del _L1_gnn_all
    return {'x': x, 'src': src, 'dst': dst, 'edge_attr_4': edge_attr_4, 'node_vec1': node_vec1, 'node_vec1_n2': node_vec1_n2, 'L1_gnn_W1': _L1_gnn_in['W1'], 'L1_gnn_b1': _L1_gnn_in['b1'], 'L1_gnn_W2': _L1_gnn_in['W2'], 'L1_gnn_b2': _L1_gnn_in['b2'], 'L1_gnn_W3': _L1_gnn_in['W3'], 'L1_gnn_b3': _L1_gnn_in['b3'], 'L1_gnn_W4': _L1_gnn_in['W4'], 'L1_gnn_b4': _L1_gnn_in['b4']}

def reference(x, src, dst, edge_attr_4, node_vec1, node_vec1_n2, L1_gnn_W1, L1_gnn_b1, L1_gnn_W2, L1_gnn_b2, L1_gnn_W3, L1_gnn_b3, L1_gnn_W4, L1_gnn_b4):
    import jax
    import jax.numpy as jnp

    def _L0_gnn_ref(src_feats, cj, ci, src_idx, dst_idx):
        import jax, jax.numpy as jnp
        import numpy as np
        N_NODES = 12500
        N_EDGES = 200000
        D_FEAT = 32
        weighted = src_feats * cj
        msgs = weighted[src_idx]
        agg = jax.ops.segment_sum(msgs, dst_idx, num_segments=N_NODES)
        return agg * ci

    def _L1_gnn_ref(x, edge_index, edge_attr, W1, b1, W2, b2, W3, b3, W4, b4):
        import jax, jax.numpy as jnp
        import numpy as np
        N_NODES = 12500
        N_EDGES = 200000
        IN_DIM = 32
        HID = 64
        OUT_DIM = 32
        EDGE_DIM = 4
        j_idx = edge_index[0]
        i_idx = edge_index[1]
        x_j = x[j_idx]
        x_i = x[i_idx]
        msg = jnp.concatenate([x_i, x_j - x_i], axis=-1)
        h = jax.nn.relu(msg @ W1 + b1)
        h = jax.nn.relu(h @ W2 + b2)
        h = jax.nn.relu(h @ W3 + b3)
        m = h @ W4 + b4
        s = jax.ops.segment_sum(m, i_idx, num_segments=N_NODES)
        cnt = jax.ops.segment_sum(jnp.ones((m.shape[0],), m.dtype), i_idx, num_segments=N_NODES)
        return s / jnp.maximum(cnt, 1.0)[:, None]
    edge_index = jnp.stack([src, dst])
    h = jnp.maximum(_layernorm(x, axis=-1), 0.0)
    x = x + _L0_gnn_ref(h, node_vec1, node_vec1_n2, src, dst)
    h = jnp.maximum(_layernorm(x, axis=-1), 0.0)
    x = x + _L1_gnn_ref(h, edge_index, edge_attr_4, L1_gnn_W1, L1_gnn_b1, L1_gnn_W2, L1_gnn_b2, L1_gnn_W3, L1_gnn_b3, L1_gnn_W4, L1_gnn_b4)
    return x

_drawn_inputs = setup_inputs


def setup_inputs(seed=0):
    import zlib

    import numpy as np

    out = dict(_drawn_inputs(seed))
    spreads = {}
    factors = {'L1_gnn_W1': 8.0,
     'L1_gnn_b1': 8.0,
     'L1_gnn_W2': 8.0,
     'L1_gnn_b2': 8.0,
     'L1_gnn_W3': 8.0,
     'L1_gnn_b3': 32.806,
     'L1_gnn_W4': 6.925,
     'L1_gnn_b4': 78.385}
    for name, (base, spread) in spreads.items():
        noise = np.random.default_rng([zlib.crc32(name.encode()), seed]).standard_normal(out[name].shape)
        drawn = base * np.exp(spread * noise) if base else spread * noise
        out[name] = jnp.asarray(drawn.astype(out[name].dtype))
    for name, factor in factors.items():
        out[name] = (out[name] * factor).astype(out[name].dtype)
    return out
```

```python
from contextlib import ExitStack

import concourse.bass as bass
from concourse import mybir

ALU = mybir.AluOpType
ACT = mybir.ActivationFunctionType
AX = mybir.AxisListType
F32 = mybir.dt.float32
BF16 = mybir.dt.bfloat16
I32 = mybir.dt.int32
I16 = mybir.dt.int16

P = 128
N = 12500
E = 200000
D = 32
H = 64
H2 = 2 * H
NP = 125
NT = N // NP
WIN = P
SUB = 4
GE = SUB * P
RING = 4
NG = -(-E // (GE * RING)) * RING
NIT = NG // RING
NSUB = NG * SUB
PADE = NSUB * P - E
NBLK = -(-NSUB // P)
LASTQ = NSUB - (NBLK - 1) * P
REALQ = (E - (NBLK - 1) * P * P) // P
REALR = E - (NBLK - 1) * P * P - REALQ * P
GB = P // SUB
EPS = 1e-5


def slot(u, lag):
    return (u - lag) % RING


class Turn:

    def __init__(self, number, i, earlier):
        self.number = number
        self.group = i * RING
        self.before = earlier + i

    def valid(self, u, lag):
        return self.number is None or 0 <= RING * self.number + u - lag < NG


def run_steps(eng, step, head, tail, sweep):
    earlier = sweep * NIT
    for u in range(RING - head, RING):
        step(Turn(-1, -1, earlier), u)
    for u in range(RING):
        step(Turn(0, 0, earlier), u)
    with eng.Fori(1, NIT - 1) as i:
        for u in range(RING):
            step(Turn(None, i, earlier), u)
    for u in range(RING):
        step(Turn(NIT - 1, NIT - 1, earlier), u)
    for u in range(tail):
        step(Turn(NIT, NIT, earlier), u)


def wait_slot(eng, sems, i, u, lag, unit=1, behind=0):
    c = (u - lag) // RING + 1 - behind
    if i.number is not None and i.number + c <= 0:
        return
    eng.wait_ge(sems[slot(u, lag)], (i.before + c) * unit)


def build(nc, x, src, dst, nv1, nv2, W1, b1, W2, b2, W3, b3, W4, b4, out):
    ctx = ExitStack()
    with ctx:
        def sb(name, shape, dt=F32):
            return ctx.enter_context(nc.sbuf_tensor(name, shape, dt))

        def ps(name, shape, dt=F32):
            return ctx.enter_context(nc.psum_tensor(name, shape, dt))

        def sem(name):
            return ctx.enter_context(nc.semaphore(name))

        def ring(name):
            return [sem(f"{name}{u}") for u in range(RING)]

        wtab = nc.dram_tensor("wtab", [N, D], F32).ap()
        qtab = nc.dram_tensor("qtab", [N, H], F32).ap()
        ptab = nc.dram_tensor("ptab", [N + WIN, H], F32).ap()
        gmin_d = nc.dram_tensor("gmin_d", [NBLK * GB], F32).ap()
        gmax_d = nc.dram_tensor("gmax_d", [NBLK * GB], F32).ap()
        rel_d = nc.dram_tensor("rel_d", [NSUB, P], I16).ap()

        xs = sb("xs", [NP, NT, D])
        scratch = sb("scratch", [P, NT * D])
        tmp = scratch[0:NP, :].rearrange("p (t d) -> p t d", d=D)
        sq = sb("sq", [NP, NT, D])
        n1 = sb("n1", [NP, NT])
        n2 = sb("n2", [NP, NT])
        mu = sb("mu", [NP, NT])
        var = sb("var", [NP, NT])
        std = sb("std", [NP, NT])
        rstd = sb("rstd", [NP, NT])
        epsc = sb("epsc", [P, 1])
        acc = sb("acc", [H + 1, N + WIN])
        ident = sb("ident", [P, P])
        iota_i = sb("iota_i", [P, P], I32)
        iota_f = sb("iota_f", [P, P])
        colid_i = sb("colid_i", [P, 1], I32)
        colid = sb("colid", [P, 1])
        dstT = sb("dstT", [P, NSUB])
        srcT = sb("srcT", [P, NSUB], I32)
        relT = sb("relT", [P, NSUB])
        rmm = sb("rmm", [P, 2, NBLK])
        gmm = sb("gmm", [NBLK, 2, GB])
        base0 = sb("base0", [P, NG])
        gtop = sb("gtop", [P, NG])
        base_f = sb("base_f", [P, NG])
        base_c = sb("base_c", [P, NG])
        base_i = sb("base_i", [P, NG], I32)
        base_row = sb("base_row", [P, NBLK])
        span = sb("span", [P, 1])
        span_i = sb("span_i", [P, 1], I32)
        idx = sb("idx", [P, RING, SUB], I32)
        pst = sb("pst", [NP + 3, NT, H])
        raw = pst[:, :, :].rearrange("p a b -> p (a b)")
        dst_i = raw[:, 0:NBLK * P].bitcast(I32).rearrange("p (b e) -> p b e", e=P)
        src_i = raw[:, NBLK * P:2 * NBLK * P].bitcast(I32).rearrange("p (b e) -> p b e", e=P)
        qst = sb("qst", [NP + 3, NT, H])
        rawq = qst[:, :, :].rearrange("p a b -> p (a b)")
        dst_r = rawq[:, 0:NBLK * P].rearrange("p (b e) -> p b e", e=P)
        src_r = rawq[:, NBLK * P:2 * NBLK * P].rearrange("p (b e) -> p b e", e=P)
        rel_r = rawq[:, 2 * NBLK * P:2 * NBLK * P + NBLK * P // 2].bitcast(I16)\
            .rearrange("p (b e) -> p b e", e=P)
        wrow = sb("wrow", [P, RING, SUB, D])
        qrow = sb("qrow", [P, RING, SUB, H])
        pwin = sb("pwin", [P, RING, H])
        relb = sb("relb", [P, RING, GE], I16)
        S = scratch[:, 0:RING * GE].rearrange("p (r k w) -> p r k w", r=RING, k=SUB)
        ST = sb("ST", [P, RING, GE])
        h1 = sb("h1", [H, 2, GE])
        h2 = sb("h2", [H2, 2, GE])
        h3 = sb("h3", [P, 2, SUB, H + 1])
        w1a = sb("w1a", [P, H])
        w1b = sb("w1b", [P, H])
        wpq = sb("wpq", [P, SUB, 2 * H])
        b1b = sb("b1b", [NP, H])
        w2s = sb("w2s", [H, H2])
        b2c = sb("b2c", [H2, 1])
        w3s = sb("w3s", [H2, H])
        b3r = sb("b3r", [3, H])
        b3p = sb("b3p", [3, 3, H], BF16)
        b3l = sb("b3l", [3, 3, H])
        b3s = sb("b3s", [3, SUB, H], BF16)
        ones3 = sb("ones3", [3, P], BF16)
        w4s = sb("w4s", [H + 1, D + 1])
        hT = sb("hT", [P, 2, NP])
        cnt = sb("cnt", [NP, NT])
        zrow = sb("zrow", [P, H])

        bank = [ps(f"bank{n}", [P, 512]) for n in range(8)]

        x_in, e_in, w_in, p0_in = sem("x_in"), sem("e_in"), sem("w_in"), sem("p0_in")
        const = sem("const")
        dve = sem("dve")
        act = sem("act")
        pe = sem("pe")
        g_out, g_in, rel_out = sem("g_out"), sem("g_in"), sem("rel_out")
        wtab_out, ptab_out, qtab_out, z_out = sem("wtab_out"), sem("ptab_out"), sem("qtab_out"), sem("z_out")
        go = [sem("go0"), sem("go1")]
        done = [sem("done0"), sem("done1")]
        fin, out_s = sem("fin"), sem("out_s")
        idx_ready, gathered, built, sums, added = (
            [ring(f"{n}_{l}_") for l in range(2)] for n in ("idx", "gath", "built", "sums", "added"))
        opened = [sem("opened0"), sem("opened1")]
        windows = [sem("windows0"), sem("windows1")]
        s_built = ring("s_built")
        rel_in, pwin_in = ring("rel_in"), ring("pwin_in")
        pre1, pre2, pre3 = ring("pre1_"), ring("pre2_"), ring("pre3_")
        act1, act2, act3 = ring("act1_"), ring("act2_"), ring("act3_")

        def bc(ap, n):
            return ap.unsqueeze(2).to_broadcast([ap.shape[0], ap.shape[1], n])

        at = {}
        at["pe_agg"] = 1 + 2 * -(-NBLK // (512 // P)) + 1
        at["pe_hT"] = at["pe_agg"] + -(-NT // (512 // D))
        at["pe_out"] = at["pe_hT"] + 2 * (NT // SUB)
        at["act_q"] = 3

        xd = x.rearrange("(p t) d -> p t d", t=NT)
        od = out.rearrange("(p t) d -> p t d", t=NT)
        SPLIT = NP // 16 * 16
        PARTS = [(0, SPLIT), (SPLIT, NP)]

        def nsweeps(eng):
            s = eng.value_load(span_i[0:1, 0:1], min_val=1, max_val=NP)
            return s

        block = ctx.enter_context(nc.Block())

        @block.vector
        def _(v):
            n = [0]

            def link(ins):
                n[0] += 1
                ins.then_inc(dve, 1)

            def settle():
                v.wait_ge(dve, n[0])

            def layernorm(scale, dest):
                link(nc.vector.tensor_reduce(mu[:, :], xs[:, :, :], AX.X, ALU.add))
                settle()
                link(nc.vector.tensor_scalar(mu[:, :], mu[:, :], 1.0 / D, None, ALU.mult))
                settle()
                link(nc.vector.tensor_tensor(tmp[:, :, :], xs[:, :, :], bc(mu[:, :], D), ALU.subtract))
                settle()
                link(nc.vector.tensor_tensor(sq[:, :, :], tmp[:, :, :], tmp[:, :, :], ALU.mult))
                settle()
                link(nc.vector.tensor_reduce(var[:, :], sq[:, :, :], AX.X, ALU.add))
                at["var"] = at.get("var", []) + [n[0]]
                v.wait_ge(act, len(at["var"]))
                link(nc.vector.reciprocal(rstd[:, :], std[:, :]))
                settle()
                link(nc.vector.tensor_tensor(tmp[:, :, :], tmp[:, :, :], bc(rstd[:, :], D), ALU.mult))
                settle()
                if scale is None:
                    link(nc.vector.tensor_scalar(dest[:, :, :], tmp[:, :, :], 0.0, None, ALU.max))
                else:
                    link(nc.vector.scalar_tensor_tensor(dest[:, :, :], tmp[:, :, :], 0.0, bc(scale[:, :], D),
                                                        ALU.max, ALU.mult))

            def sweep_start(l, s):
                nc.vector.tensor_tensor(relT[:, :].rearrange("p (g k) -> p g k", k=SUB),
                                        dstT[:, :].rearrange("p (g k) -> p g k", k=SUB),
                                        bc(base_f[:, :], SUB), ALU.subtract).then_inc(windows[l], 1)
                nc.vector.tensor_scalar(base_c[:, :], base_f[:, :], float(N), None, ALU.min).then_inc(windows[l], 1)
                v.wait_ge(windows[l], s * 7 + 2)
                c = E // P
                nc.vector.memset(relT[:, c + 1:NSUB], -1.0).then_inc(windows[l], 1)
                nc.vector.memset(relT[E - c * P:P, c:c + 1], -1.0).then_inc(windows[l], 1)
                nc.vector.tensor_copy(base_i[:, :], base_c[:, :]).then_inc(windows[l], 1)
                v.wait_ge(windows[l], s * 7 + 5)
                v.sem_inc(go[l], 1)

            def sweep_end(l, s):
                for u in range(RING):
                    v.wait_ge(added[l][u], (s + 1) * NIT)
                nc.vector.tensor_scalar(base_f[:, :], base_f[:, :], float(WIN), None, ALU.add)\
                    .then_inc(windows[l], 1)
                nc.vector.tensor_scalar(colid[:, :], colid[:, :], float(WIN), None, ALU.add)\
                    .then_inc(windows[l], 1)
                v.wait_ge(windows[l], s * 7 + 7)

            def copy_index(l, i, u):
                if i.valid(u, -3):
                    wait_slot(v, gathered[l], i, u, -3, 16 * SUB, 1)
                    g = i.group + u + 3
                    nc.vector.tensor_copy(idx[:, slot(u, -3), :], srcT[:, bass.ds(g * SUB, SUB)])\
                        .then_inc(idx_ready[l][slot(u, -3)], 1)

            def build_S(l, sems, i, u):
                wait_slot(v, sums[l], i, u, 0, 1, 1)
                g = i.group + u
                nc.vector.tensor_tensor(
                    S[:, u, :, :], iota_f[:, :].unsqueeze(1).to_broadcast([P, SUB, WIN]),
                    bc(relT[:, bass.ds(g * SUB, SUB)], WIN), ALU.is_equal).then_inc(sems[u], 1)

            def add_sums(l, rows, banks, i, u, lag):
                if not i.valid(u, lag):
                    return
                base = v.value_load(base_i[0:1, bass.ds(i.group + u - lag, 1)], min_val=0, max_val=N)
                wait_slot(v, sums[l], i, u, lag)
                wait_slot(v, added[l], i, u, lag + 1)
                s = slot(u, lag)
                nc.vector.tensor_tensor(acc[0:rows, bass.ds(base, WIN)], acc[0:rows, bass.ds(base, WIN)],
                                        banks[s % 2][0:rows, 0:WIN], ALU.add).then_inc(added[l][s], 1)

            v.wait_ge(const, 2)
            link(nc.vector.tensor_copy(iota_f[:, :], iota_i[:, :]))
            link(nc.vector.tensor_copy(colid[:, :], colid_i[:, :]))
            link(nc.vector.memset(epsc[:, :], EPS))
            link(nc.vector.memset(rmm[:, :, :], 0.0))
            link(nc.vector.memset(acc[:, :], 0.0))
            link(nc.vector.memset(ones3[:, :], 1.0))
            link(nc.vector.memset(h3[:, :, :, H:H + 1], 1.0))
            link(nc.vector.memset(w4s[:, :], 0.0))
            link(nc.vector.memset(wpq[:, :, :], 0.0))
            link(nc.vector.memset(zrow[:, :], 0.0))
            settle()
            link(nc.vector.memset(w4s[H:H + 1, D:D + 1], 1.0))
            at["zeros"] = n[0]
            v.wait_ge(e_in, 16 * 10)
            last = NBLK - 1
            link(nc.vector.tensor_copy(dst_r[:, 0:last, :], dst_i[:, 0:last, :]))
            link(nc.vector.tensor_copy(dst_r[0:LASTQ, last, :], dst_i[0:LASTQ, last, :]))
            at["dst_r"] = n[0]
            settle()
            for m, op in enumerate((ALU.min, ALU.max)):
                link(nc.vector.tensor_reduce(rmm[:, m, 0:last], dst_r[:, 0:last, :], AX.X, op))
                link(nc.vector.tensor_reduce(rmm[0:LASTQ, m, last:NBLK], dst_r[0:LASTQ, last:NBLK, :], AX.X, op))
            at["rmm"] = n[0]
            link(nc.vector.tensor_copy(src_r[:, 0:last, :], src_i[:, 0:last, :]))
            link(nc.vector.tensor_copy(src_r[0:LASTQ, last, :], src_i[0:LASTQ, last, :]))
            at["src_r"] = n[0]
            v.wait_ge(pe, 1)
            for m, op in enumerate((ALU.min, ALU.max)):
                link(nc.vector.tensor_reduce(
                    gmm[:, m, :], bank[m][0:NBLK, 0:P].rearrange("b (g k) -> b g k", k=SUB), AX.X, op))
            at["gmm"] = n[0]
            per = 512 // P
            for k in range(-(-NBLK // per)):
                a, b = k * 512, min((k + 1) * 512, NSUB)
                v.wait_ge(pe, 2 + k)
                link(nc.vector.tensor_copy(dstT[:, a:b], bank[2 + k % 2][:, 0:b - a]))
                at[("dstT", k)] = n[0]
            for k in range(-(-NBLK // per)):
                a, b = k * 512, min((k + 1) * 512, NSUB)
                v.wait_ge(pe, 2 + -(-NBLK // per) + k)
                link(nc.vector.tensor_copy(srcT[:, a:b], bank[2 + k % 2][:, 0:b - a]))
                at[("srcT", k)] = n[0]
            v.wait_ge(x_in, 16 * 6)
            layernorm(n1, sq)
            at["w"] = n[0]
            v.wait_ge(g_in, 16 * 6)
            link(nc.vector.tensor_tensor(gtop[:, :], gtop[:, :], base0[:, :], ALU.subtract))
            link(nc.vector.tensor_copy(base_f[:, :], base0[:, :]))
            link(nc.vector.tensor_tensor(rel_r[:, 0:last, :], dst_r[:, 0:last, :],
                                         bc(base_row[:, 0:last], P), ALU.subtract))
            link(nc.vector.tensor_tensor(rel_r[0:LASTQ, last:NBLK, :], dst_r[0:LASTQ, last:NBLK, :],
                                         bc(base_row[0:LASTQ, last:NBLK], P), ALU.subtract))
            at["rel_r"] = n[0]
            settle()
            link(nc.vector.tensor_reduce(span[:, :], gtop[:, :], AX.X, ALU.max))
            settle()
            link(nc.vector.tensor_copy(span_i[:, :], span[:, :]))
            settle()
            link(nc.vector.tensor_scalar(span_i[:, :], span_i[:, :], 7, None, ALU.arith_shift_right))
            settle()
            link(nc.vector.tensor_scalar(span_i[:, :], span_i[:, :], 1, None, ALU.add))
            settle()
            at["span"] = n[0]

            def step0(i, u):
                copy_index(0, i, u)
                if i.valid(u, 0):
                    build_S(0, built[0], i, u)
                add_sums(0, D, [bank[0], bank[1]], i, u, 2)

            with v.Fori(0, nsweeps(v)) as s:
                sweep_start(0, s)
                run_steps(v, step0, 3, 2, s)
                sweep_end(0, s)
            v.sem_inc(done[0], 1)
            link(nc.vector.tensor_copy(base_f[:, :], base0[:, :]))
            link(nc.vector.tensor_copy(colid[:, :], colid_i[:, :]))

            per_bank = 512 // D
            for k in range(-(-NT // per_bank)):
                a, b = k * per_bank, min((k + 1) * per_bank, NT)
                v.wait_ge(pe, at["pe_agg"] + k)
                link(nc.vector.tensor_tensor(
                    tmp[:, a:b, :], bank[2 + k % 2][0:NP, 0:(b - a) * D].rearrange("p (t d) -> p t d", d=D),
                    bc(n2[:, a:b], D), ALU.mult))
                at[("agg", k)] = n[0]
            settle()
            link(nc.vector.memset(acc[:, :], 0.0))
            at["acc_zero"] = n[0]
            link(nc.vector.tensor_tensor(xs[:, :, :], xs[:, :, :], tmp[:, :, :], ALU.add))
            settle()
            layernorm(None, sq)
            at["h"] = n[0]

            v.wait_ge(w_in, 16 * 15)
            for k in range(SUB):
                r = slice(k * D, (k + 1) * D)
                link(nc.vector.tensor_tensor(wpq[r, k, 0:H], w1a[r, :], w1b[r, :], ALU.subtract))
                link(nc.vector.tensor_copy(wpq[r, k, H:2 * H], w1b[r, :]))
            at["wpq"] = n[0]
            for k in range(3):
                link(nc.vector.tensor_copy(b3p[:, k, :], b3r[:, :]))
                settle()
                link(nc.vector.tensor_tensor(b3r[:, :], b3r[:, :], b3p[:, k, :], ALU.subtract))
                settle()
            link(nc.vector.tensor_tensor(b3l[:, :, :], b3p[:, :, :], bc(ident[0:3, 0:3], H), ALU.mult))
            settle()
            link(nc.vector.tensor_tensor(b3l[:, 0, :], b3l[:, 0, :], b3l[:, 1, :], ALU.add))
            settle()
            link(nc.vector.tensor_tensor(b3s[:, 0, :], b3l[:, 0, :], b3l[:, 2, :], ALU.add))
            settle()
            for k in range(1, SUB):
                link(nc.vector.tensor_copy(b3s[:, k, :], b3s[:, 0, :]))
            at["b3s"] = n[0]

            for k in range(NT // SUB):
                v.wait_ge(pe, at["pe_hT"] + 2 * k)
                if k >= 2:
                    v.wait_ge(pe, at["pe_hT"] + 2 * (k - 2) + 1)
                link(nc.vector.tensor_copy(hT[:, k % 2, :], bank[2 + k % 2][:, 0:NP]))
                at[("hT", k)] = n[0]
                if k >= 1:
                    v.wait_ge(pe, at["pe_hT"] + 2 * (k - 1) + 1)
                    o = bank[4 + (k - 1) % 2][0:NP, :].rearrange("p (t c) -> p t c", c=2 * H)
                    link(nc.vector.tensor_tensor(pst[0:NP, SUB * (k - 1):SUB * k, :], o[:, :, 0:H],
                                                 b1b[:, :].unsqueeze(1).to_broadcast([NP, SUB, H]), ALU.add))
                    at[("P", k - 1)] = n[0]
            k = NT // SUB
            v.wait_ge(pe, at["pe_hT"] + 2 * (k - 1) + 1)
            o = bank[4 + (k - 1) % 2][0:NP, :].rearrange("p (t c) -> p t c", c=2 * H)
            link(nc.vector.tensor_tensor(pst[0:NP, SUB * (k - 1):SUB * k, :], o[:, :, 0:H],
                                         b1b[:, :].unsqueeze(1).to_broadcast([NP, SUB, H]), ALU.add))
            at[("P", k - 1)] = n[0]

            def step1(i, u):
                copy_index(1, i, u)
                if i.valid(u, 0):
                    build_S(1, s_built, i, u)
                    wait_slot(v, rel_in, i, u, 0, 16)
                    wait_slot(v, pre1, i, u, 0, 1, 1)
                    nc.vector.tensor_scalar(ST[:, u, :], relb[:, u, :], colid[:, 0:1], None, ALU.is_equal)\
                        .then_inc(built[1][u], 1)
                if i.valid(u, 3):
                    s3 = slot(u, 3)
                    wait_slot(v, pre3, i, u, 3)
                    wait_slot(v, sums[1], i, u, 5)
                    nc.vector.tensor_scalar(
                        h3[:, s3 % 2, :, 0:H], bank[4 + s3 % 2][:, 0:SUB * H].rearrange("p (k f) -> p k f", f=H),
                        0.0, None, ALU.max).then_inc(act3[s3], 1)
                add_sums(1, H + 1, [bank[6], bank[7]], i, u, 4)

            with v.Fori(0, nsweeps(v)) as s:
                sweep_start(1, s)
                run_steps(v, step1, 3, 4, s)
                sweep_end(1, s)
            v.sem_inc(done[1], 1)

            per_bank = 512 // (D + 1)
            for k in range(-(-NT // per_bank)):
                a, b = k * per_bank, min((k + 1) * per_bank, NT)
                v.wait_ge(pe, at["pe_out"] + k)
                o = bank[k % 2][0:NP, 0:(b - a) * (D + 1)].rearrange("p (t c) -> p t c", c=D + 1)
                link(nc.vector.tensor_scalar(cnt[:, a:b], o[:, :, D], 1.0, None, ALU.max))
                settle()
                link(nc.vector.reciprocal(cnt[:, a:b], cnt[:, a:b]))
                settle()
                link(nc.vector.tensor_tensor(tmp[:, a:b, :], o[:, :, 0:D], bc(cnt[:, a:b], D), ALU.mult))
                at[("mean", k)] = n[0]
                settle()
                nc.vector.tensor_tensor(sq[:, a:b, :], tmp[:, a:b, :], xs[:, a:b, :], ALU.add).then_inc(fin, 1)

        @block.tensor
        def _(t):
            n = [0]

            def batch(ins):
                n[0] += 1
                ins.then_inc(pe, 1)

            per = 512 // P
            t.wait_ge(const, 3)
            t.wait_ge(dve, at["rmm"])
            for m in range(2):
                last = nc.tensor.transpose(bank[m][0:NBLK, 0:P], rmm[:, m, :], ident[:, :])
            batch(last)
            for which, rows in (("dstT", dst_r), ("srcT", src_r)):
                if which == "srcT":
                    t.wait_ge(dve, at["src_r"])
                for k in range(-(-NBLK // per)):
                    prev = (which, k - 2) if k >= 2 else (("dstT", k + 2) if which == "srcT" else None)
                    if prev:
                        t.wait_ge(dve, at[prev])
                    for b in range(k * per, min((k + 1) * per, NBLK)):
                        q = P if b < NBLK - 1 else LASTQ
                        c = (b - k * per) * P
                        last = nc.tensor.transpose(bank[2 + k % 2][:, c:c + q], rows[0:q, b, :], ident[0:q, 0:q])
                    batch(last)
            t.wait_ge(dve, at["span"])

            def step0(i, u):
                if not i.valid(u, 0):
                    return
                wait_slot(t, built[0], i, u, 0)
                wait_slot(t, gathered[0], i, u, 0, 16 * SUB)
                wait_slot(t, added[0], i, u, 2)
                for k in range(SUB):
                    last = nc.tensor.matmul(bank[u % 2][0:D, 0:WIN], wrow[:, u, k, :], S[:, u, k, :],
                                            start=(k == 0), stop=(k == SUB - 1))
                last.then_inc(sums[0][u], 1)

            with t.Fori(0, nsweeps(t)) as s:
                t.wait_ge(go[0], s + 1)
                run_steps(t, step0, 0, 0, s)
            t.wait_ge(done[0], 1)

            assert at["pe_agg"] == n[0] + 1
            per_bank = 512 // D
            accn = acc[:, 0:N].rearrange("f (p t) -> f t p", t=NT)
            for k in range(-(-NT // per_bank)):
                a, b = k * per_bank, min((k + 1) * per_bank, NT)
                if k >= 2:
                    t.wait_ge(dve, at[("agg", k - 2)])
                for c in range(a, b):
                    last = nc.tensor.matmul(bank[2 + k % 2][0:NP, (c - a) * D:(c - a + 1) * D],
                                            accn[0:D, c, :], ident[0:D, 0:D], start=True, stop=True)
                batch(last)
            assert at["pe_hT"] == n[0] + 1
            t.wait_ge(dve, at["wpq"])

            def transpose_h(k):
                if k >= 2:
                    t.wait_ge(dve, at[("hT", k - 2)])
                batch(nc.tensor.transpose(bank[2 + k % 2][:, 0:NP],
                                          sq[:, SUB * k:SUB * (k + 1), :].rearrange("p a b -> p (a b)"),
                                          ident[0:NP, 0:NP]))

            for k in range(NT // SUB):
                transpose_h(k)
                t.wait_ge(dve, at[("hT", k)])
                if k >= 2:
                    t.wait_ge(dve, at[("P", k - 2)])
                    t.wait_ge(act, at["act_q"] + k - 2)
                batch(nc.tensor.matmul(bank[4 + k % 2][0:NP, :], hT[:, k % 2, :],
                                       wpq[:, :, :].rearrange("p a b -> p (a b)"), start=True, stop=True))
            t.wait_ge(dve, at["b3s"])

            def step1(i, u):
                if i.valid(u, 0):
                    wait_slot(t, built[1], i, u, 0)
                    wait_slot(t, pwin_in, i, u, 0, 16)
                    wait_slot(t, act1, i, u, 2)
                    nc.tensor.matmul(bank[u % 2][0:H, :], pwin[:, u, :], ST[:, u, :], start=True, stop=False)
                    wait_slot(t, gathered[1], i, u, 0, 16 * SUB)
                    for k in range(SUB):
                        last = nc.tensor.matmul(bank[u % 2][0:H, k * P:(k + 1) * P], qrow[:, u, k, :],
                                                ident[:, :], start=False, stop=(k == SUB - 1))
                    last.then_inc(pre1[u], 1)
                if i.valid(u, 1):
                    s1 = slot(u, 1)
                    wait_slot(t, act1, i, u, 1)
                    wait_slot(t, act2, i, u, 3)
                    nc.tensor.matmul(bank[2 + s1 % 2][:, :], w2s[:, :], h1[:, s1 % 2, :], start=True, stop=True)\
                        .then_inc(pre2[s1], 1)
                if i.valid(u, 2):
                    s2 = slot(u, 2)
                    wait_slot(t, act2, i, u, 2)
                    wait_slot(t, act3, i, u, 4)
                    nc.tensor.matmul(bank[4 + s2 % 2][:, 0:SUB * H], ones3[:, :],
                                     b3s[:, :, :].rearrange("p a b -> p (a b)"), start=True, stop=False)
                    for k in range(SUB):
                        last = nc.tensor.matmul(bank[4 + s2 % 2][:, k * H:(k + 1) * H],
                                                h2[:, s2 % 2, k * P:(k + 1) * P], w3s[:, :],
                                                start=False, stop=(k == SUB - 1))
                    last.then_inc(pre3[s2], 1)
                if i.valid(u, 3):
                    s3 = slot(u, 3)
                    wait_slot(t, act3, i, u, 3)
                    wait_slot(t, added[1], i, u, 5)
                    for k in range(SUB):
                        last = nc.tensor.matmul(bank[6 + s3 % 2][0:H + 1, 0:WIN], h3[:, s3 % 2, k, :],
                                                S[:, s3, k, :], start=(k == 0), stop=(k == SUB - 1))
                    last.then_inc(sums[1][s3], 1)

            with t.Fori(0, nsweeps(t)) as s:
                t.wait_ge(go[1], s + 1)
                run_steps(t, step1, 0, 3, s)
            t.wait_ge(done[1], 1)

            assert at["pe_out"] == n[0] + 1
            per_bank = 512 // (D + 1)
            for k in range(-(-NT // per_bank)):
                a, b = k * per_bank, min((k + 1) * per_bank, NT)
                if k >= 2:
                    t.wait_ge(dve, at[("mean", k - 2)])
                for c in range(a, b):
                    last = nc.tensor.matmul(bank[k % 2][0:NP, (c - a) * (D + 1):(c - a + 1) * (D + 1)],
                                            accn[:, c, :], w4s[:, :], start=True, stop=True)
                batch(last)

        @block.scalar
        def _(a):
            for m in range(2):
                a.wait_ge(dve, at["var"][m])
                nc.scalar.activation(std[:, :], var[:, :], ACT.Sqrt, bias=epsc[0:NP, :], scale=1.0 / D)\
                    .then_inc(act, 1)
            assert at["act_q"] == 3
            a.wait_ge(rel_out, 32)
            for k in range(NT // SUB):
                a.wait_ge(dve, at[("P", k)])
                o = bank[4 + k % 2][0:NP, :].rearrange("p (t c) -> p t c", c=2 * H)
                nc.scalar.activation(qst[0:NP, SUB * k:SUB * (k + 1), :], o[:, :, H:2 * H], ACT.Copy)\
                    .then_inc(act, 1)

            def step1(i, u):
                if i.valid(u, 0):
                    wait_slot(a, pre1, i, u, 0)
                    wait_slot(a, pre2, i, u, 2)
                    nc.scalar.activation(h1[:, u % 2, :], bank[u % 2][0:H, :], ACT.Relu).then_inc(act1[u], 1)
                if i.valid(u, 1):
                    s1 = slot(u, 1)
                    wait_slot(a, pre2, i, u, 1)
                    wait_slot(a, pre3, i, u, 3)
                    nc.scalar.activation(h2[:, s1 % 2, :], bank[2 + s1 % 2][:, :], ACT.Relu, bias=b2c[:, 0:1])\
                        .then_inc(act2[s1], 1)

            with a.Fori(0, nsweeps(a)) as s:
                a.wait_ge(go[1], s + 1)
                run_steps(a, step1, 0, 1, s)

        @block.gpsimd
        def _(g):
            nc.gpsimd.iota(iota_i[:, :], pattern=[[1, P]], base=0, channel_multiplier=0).then_inc(const, 1)
            nc.gpsimd.iota(colid_i[:, :], pattern=[[0, 1]], base=0, channel_multiplier=1).then_inc(const, 1)
            g.wait_ge(const, 2)
            nc.gpsimd.memset(ident[:, :], 0.0).then_inc(p0_in, 1)
            g.wait_ge(p0_in, 1)
            nc.gpsimd.affine_select(out=ident[:, :], in_=ident[:, :], compare_op=ALU.not_equal, fill=1.0,
                                    base=0, pattern=[[-1, P]], channel_multiplier=1).then_inc(const, 1)


            def gathers(l, table, rows, stored):
                def step(i, u):
                    wait_slot(g, idx_ready[l], i, u, 0)
                    free = sums[0] if l == 0 else pre1
                    wait_slot(g, free, i, u, 0, 1, 1)
                    g.sem_inc(opened[l], 1)
                    g.wait_ge(stored, 32)
                    for k in range(SUB):
                        nc.gpsimd.indirect_dma_start(
                            out=rows[:, u, k, :], out_offset=None, in_=table,
                            in_offset=bass.IndirectOffsetOnAxis(ap=idx[:, u, k:k + 1], axis=0))\
                            .then_inc(gathered[l][u], 16)
                return step

            g.wait_ge(dve, at["span"])
            with g.Fori(0, nsweeps(g)) as s:
                g.wait_ge(go[0], s + 1)
                run_steps(g, gathers(0, wtab, wrow, wtab_out), 0, 0, s)
            with g.Fori(0, nsweeps(g)) as s:
                g.wait_ge(go[1], s + 1)
                run_steps(g, gathers(1, qtab, qrow, qtab_out), 0, 0, s)

        @block.sync
        def _(s_):
            full = (NBLK - 1) * P * P
            mid = full + REALQ * P
            for ids, tile_ in ((dst, dst_i), (src, src_i)):
                s_.dma_start(tile_[:, 0:NBLK - 1, :], ids[0:full].rearrange("(b q e) -> q b e", q=P, e=P))\
                    .then_inc(e_in, 16)
                s_.dma_start(tile_[0:REALQ, NBLK - 1, :], ids[full:mid].rearrange("(q e) -> q e", e=P))\
                    .then_inc(e_in, 16)
                s_.dma_start(tile_[REALQ:REALQ + 1, NBLK - 1, 0:REALR], ids[mid:E].unsqueeze(0)).then_inc(e_in, 16)
                s_.dma_start(tile_[REALQ:REALQ + 1, NBLK - 1, REALR:P], ids[E - (P - REALR):E].unsqueeze(0))\
                    .then_inc(e_in, 16)
                k = LASTQ - REALQ - 1
                s_.dma_start(tile_[REALQ + 1:LASTQ, NBLK - 1, :],
                             ids[E - k * P:E].rearrange("(q e) -> q e", e=P)).then_inc(e_in, 16)
            for a, b in PARTS:
                s_.dma_start(xs[a:b, :, :], xd[a:b, :, :]).then_inc(x_in, 16)
                s_.dma_start(n1[a:b, :], nv1.rearrange("(p t) o -> p (t o)", t=NT)[a:b, :]).then_inc(x_in, 16)
                s_.dma_start(n2[a:b, :], nv2.rearrange("(p t) o -> p (t o)", t=NT)[a:b, :]).then_inc(x_in, 16)
            s_.wait_ge(dve, at["zeros"])
            for k in range(SUB):
                s_.dma_start(w1a[k * D:(k + 1) * D, :], W1[0:D, :]).then_inc(w_in, 16)
                s_.dma_start(w1b[k * D:(k + 1) * D, :], W1[D:2 * D, :]).then_inc(w_in, 16)
            s_.dma_start(b1b[:, :], b1.unsqueeze(0).to_broadcast([NP, H])).then_inc(w_in, 16)
            s_.dma_start(w2s[:, :], W2).then_inc(w_in, 16)
            s_.dma_start(b2c[:, :], b2.unsqueeze(1)).then_inc(w_in, 16)
            s_.dma_start(w3s[:, :], W3).then_inc(w_in, 16)
            s_.dma_start(b3r[:, :], b3.unsqueeze(0).to_broadcast([3, H])).then_inc(w_in, 16)
            s_.dma_start(w4s[0:H, 0:D], W4).then_inc(w_in, 16)
            s_.dma_start(w4s[H:H + 1, 0:D], b4.unsqueeze(0)).then_inc(w_in, 16)
            s_.dma_start(ptab[N:N + WIN, :], zrow[:, :]).then_inc(z_out, 16)
            s_.wait_ge(dve, at["gmm"])
            s_.dma_start(gmin_d.rearrange("(b g) -> b g", g=GB), gmm[:, 0, :]).then_inc(g_out, 16)
            s_.dma_start(gmax_d.rearrange("(b g) -> b g", g=GB), gmm[:, 1, :]).then_inc(g_out, 16)
            s_.wait_ge(g_out, 32)
            s_.dma_start(base0[:, :], gmin_d[0:NG].unsqueeze(0).to_broadcast([P, NG])).then_inc(g_in, 16)
            s_.dma_start(gtop[:, :], gmax_d[0:NG].unsqueeze(0).to_broadcast([P, NG])).then_inc(g_in, 16)
            for r in range(SUB):
                s_.dma_start(base_row[r:P:SUB, :], gmin_d.rearrange("(b g) -> g b", g=GB),
                             allow_slow_non_contiguous=True).then_inc(g_in, 16)
            s_.wait_ge(dve, at["w"])
            wd = wtab.rearrange("(p t) d -> p t d", t=NT)
            for a, b in PARTS:
                s_.dma_start(wd[a:b, :, :], sq[a:b, :, :]).then_inc(wtab_out, 16)
            s_.wait_ge(dve, at["rel_r"])
            s_.dma_start(rel_d[0:(NBLK - 1) * P, :].rearrange("(b q) e -> q b e", q=P), rel_r[:, 0:NBLK - 1, :])\
                .then_inc(rel_out, 16)
            s_.dma_start(rel_d[(NBLK - 1) * P:NSUB, :], rel_r[0:LASTQ, NBLK - 1, :]).then_inc(rel_out, 16)
            pd = ptab[0:N, :].rearrange("(p t) d -> p t d", t=NT)
            qd = qtab.rearrange("(p t) d -> p t d", t=NT)
            s_.wait_ge(act, at["act_q"] + NT // SUB - 1)
            for a, b in PARTS:
                s_.dma_start(qd[a:b, :, :], qst[a:b, :, :]).then_inc(qtab_out, 16)
            s_.wait_ge(dve, at[("P", NT // SUB - 1)])
            for a, b in PARTS:
                s_.dma_start(pd[a:b, :, :], pst[a:b, :, :]).then_inc(ptab_out, 16)
            s_.wait_ge(z_out, 16)
            s_.wait_ge(rel_out, 32)
            s_.wait_ge(ptab_out, 32)

            relg = rel_d.rearrange("(g k) e -> g (k e)", k=SUB)

            def step1(i, u):
                g = i.group + u
                wait_slot(s_, built[1], i, u, 0, 1, 1)
                s_.dma_start(relb[:, u, :], relg[bass.ds(g, 1), :].to_broadcast([P, GE]))\
                    .then_inc(rel_in[u], 16)
                base = s_.value_load(base_i[0:1, bass.ds(g, 1)], min_val=0, max_val=N)
                wait_slot(s_, pre1, i, u, 0, 1, 1)
                s_.dma_start(pwin[:, u, :], ptab[bass.ds(base, WIN), :]).then_inc(pwin_in[u], 16)

            with s_.Fori(0, nsweeps(s_)) as s:
                s_.wait_ge(go[1], s + 1)
                run_steps(s_, step1, 0, 0, s)

            per_bank = 512 // (D + 1)
            s_.wait_ge(fin, -(-NT // per_bank))
            for a, b in PARTS:
                s_.dma_start(od[a:b, :, :], sq[a:b, :, :]).then_inc(out_s, 16)
            s_.wait_ge(out_s, 32)


_INS = ["x", "src", "dst", "node_vec1", "node_vec1_n2", "L1_gnn_W1", "L1_gnn_b1", "L1_gnn_W2", "L1_gnn_b2",
        "L1_gnn_W3", "L1_gnn_b3", "L1_gnn_W4", "L1_gnn_b4"]


def kernel(**inputs):
    import numpy as _np
    import concourse.bacc as _bacc
    from concourse import mybir as _mybir
    from concourse.bass_utils import run_bass_kernel_spmd as _run

    nc = _bacc.Bacc("TRN2", target_bir_lowering=False, num_devices=1)
    arrays, args = {}, []
    for name in _INS:
        a = _np.ascontiguousarray(inputs[name])
        arrays[f"in_{name}_dram"] = a
        args.append(nc.dram_tensor(f"in_{name}_dram", a.shape, _mybir.dt.from_np(a.dtype), kind="ExternalInput").ap())
    args.append(nc.dram_tensor("out_dram", (N, D), _mybir.dt.float32, kind="ExternalOutput").ap())
    build(nc, *args)
    r = _run(nc, [arrays], core_ids=[0])
    return r.results[0]["out_dram"]
```

```python
from contextlib import ExitStack

import concourse.bass as bass
from concourse import mybir

ALU = mybir.AluOpType
ACT = mybir.ActivationFunctionType
AX = mybir.AxisListType
F32 = mybir.dt.float32
BF16 = mybir.dt.bfloat16
I32 = mybir.dt.int32
I16 = mybir.dt.int16
F32R = mybir.dt.float32r

P = 128
N = 12500
E = 200000
D = 32
H = 64
H2 = 2 * H
NP = 125
NT = N // NP
WIN = P
SUB = 4
GE = SUB * P
RING = 8
DEEP = 4
LEAD = 7
NG = -(-E // (GE * RING)) * RING
NIT = NG // RING
NSUB = NG * SUB
PADE = NSUB * P - E
NBLK = -(-NSUB // P)
LASTQ = NSUB - (NBLK - 1) * P
REALQ = (E - (NBLK - 1) * P * P) // P
REALR = E - (NBLK - 1) * P * P - REALQ * P
GB = P // SUB
EPS = 1e-5
CT = 20
NC = NT // CT
TC = P // D
STAGES = 5
OT = 512 // D
NOUT = -(-NT // OT)


def slot(u, lag):
    return (u - lag) % RING


class Turn:

    def __init__(self, number, i, earlier):
        self.number = number
        self.group = i * RING
        self.before = earlier + i

    def valid(self, u, lag):
        return self.number is None or 0 <= RING * self.number + u - lag < NG


def run_steps(eng, step, head, tail, sweep):
    earlier = sweep * NIT
    for u in range(RING - head, RING):
        step(Turn(-1, -1, earlier), u)
    for u in range(RING):
        step(Turn(0, 0, earlier), u)
    with eng.Fori(1, NIT - 1) as i:
        for u in range(RING):
            step(Turn(None, i, earlier), u)
    for u in range(RING):
        step(Turn(NIT - 1, NIT - 1, earlier), u)
    for u in range(tail):
        step(Turn(NIT, NIT, earlier), u)


def wait_slot(eng, sems, i, u, lag, unit=1):
    r = len(sems)
    c = (u - lag) // r + 1
    if i.number is not None and i.number * (RING // r) + c <= 0:
        return
    eng.wait_ge(sems[(u - lag) % r], (i.before * (RING // r) + c) * unit)


def build(nc, x, src, dst, nv1, nv2, W1, b1, W2, b2, W3, b3, W4, b4, out):
    ctx = ExitStack()
    with ctx:
        def sb(name, shape, dt=F32):
            return ctx.enter_context(nc.sbuf_tensor(name, shape, dt))

        def sem(name):
            return ctx.enter_context(nc.semaphore(name))

        def ring(name, n=DEEP):
            return [sem(f"{name}{u}") for u in range(n)]

        wtab = nc.dram_tensor("wtab", [N, 2 * D], F32).ap()
        qtab = nc.dram_tensor("qtab", [N, 2 * H], F32).ap()
        ptab = nc.dram_tensor("ptab", [N + WIN, 2 * H], F32).ap()
        gmin_d = nc.dram_tensor("gmin_d", [NBLK * GB], F32).ap()
        gmax_d = nc.dram_tensor("gmax_d", [NBLK * GB], F32).ap()
        rel_d = nc.dram_tensor("rel_d", [NSUB, P], I16).ap()

        xs = sb("xs", [NP, NT, D])
        tmp = sb("tmp", [NP, NT, D])
        sq = sb("sq", [NP, NT, D])
        n1 = sb("n1", [NP, NT])
        n2 = sb("n2", [NP, NT])
        mu = sb("mu", [NP, NT])
        var = sb("var", [NP, NT])
        std = sb("std", [NP, NT])
        rstd = sb("rstd", [NP, NT])
        deg = sb("deg", [NP, NT])
        rdeg = sb("rdeg", [NP, NT])
        has = sb("has", [NP, NT])
        epsc = sb("epsc", [P, 1])
        acc = sb("acc", [P, N + WIN])
        ident = sb("ident", [P, P])
        identr = sb("identr", [P, P], F32R)
        iota_i = sb("iota_i", [P, P], I32)
        iota_f = sb("iota_f", [P, P])
        negid_i = sb("negid_i", [P, 1], I32)
        negid = sb("negid", [P, 1])
        zrow = sb("zrow", [P, 2 * H])
        ones3 = sb("ones3", [3, P], BF16)
        dstT = sb("dstT", [P, NSUB])
        srcT = sb("srcT", [P, NSUB], I32)
        relT = sb("relT", [P, NSUB])
        rmm = sb("rmm", [P, 2, NBLK])
        gmm = sb("gmm", [NBLK, 2, GB])
        base0 = sb("base0", [P, NG])
        gtop = sb("gtop", [P, NG])
        base_f = sb("base_f", [P, NG])
        base_i = sb("base_i", [P, NG], I32)
        base_row = sb("base_row", [P, NBLK])
        span = sb("span", [P, 1])
        span_i = sb("span_i", [P, 1], I32)
        idx = sb("idx", [P, RING, SUB], I32)
        BW = NBLK * P
        raw = sb("raw", [P, max(2 * BW + BW // 2, STAGES * TC * 4 * H)])
        dst_r, src_r = (raw[:, k * BW:(k + 1) * BW].rearrange("p (b e) -> p b e", e=P) for k in range(2))
        dst_i, src_i = (r.bitcast(I32) for r in (dst_r, src_r))
        rel_r = raw[:, 2 * BW:2 * BW + BW // 2].bitcast(I16).rearrange("p (b e) -> p b e", e=P)
        stage = raw[0:NP, 0:STAGES * TC * 4 * H].bitcast(F32R)\
            .rearrange("p (s t c h) -> p s t c h", s=STAGES, t=TC, c=4)
        wrow = sb("wrow", [P, RING, SUB, 2 * D + 2], F32R)
        S = sb("S", [P, DEEP, SUB, WIN], F32R)
        relb = sb("relb", [P, DEEP, GE], I16)
        RW = 2 * H + 2
        sizes = [RING * SUB * RW, DEEP * GE, DEEP * RW, 2 * SUB * 2 * H]
        starts = [sum(sizes[:k]) for k in range(len(sizes) + 1)]
        l1buf = sb("l1buf", [P, max(starts[-1], NT * 2 * D)], F32R)
        qrow, ST, pwin, h3 = (l1buf[:, a:b] for a, b in zip(starts, starts[1:]))
        qrow = qrow.rearrange("p (r k c) -> p r k c", r=RING, k=SUB)
        ST = ST.rearrange("p (r e) -> p r e", r=DEEP)
        pwin = pwin.rearrange("p (r c) -> p r c", r=DEEP)
        h3 = h3.rearrange("p (r k c) -> p r k c", r=2, k=SUB)
        wst = l1buf[0:NP, 0:NT * 2 * D].rearrange("p (t c d) -> p t c d", t=NT, c=2)
        h1 = sb("h1", [H, 2, GE])
        h2 = sb("h2", [H2, 2, GE])
        w1a = sb("w1a", [P, H])
        w1b = sb("w1b", [P, H])
        wpq = sb("wpq", [P, TC, 2 * H])
        w2s = sb("w2s", [H, H2])
        b2c = sb("b2c", [H2, 1])
        w3s = sb("w3s", [H2, H])
        brow = sb("brow", [3, 2, H])
        bpart = sb("bpart", [3, 3, 2, H], BF16)
        bmask = sb("bmask", [3, 3, 2, H])
        b1s = sb("b1s", [3, TC, 2 * H], BF16)
        b3s = sb("b3s", [3, SUB, H], BF16)
        w4s = sb("w4s", [P, D])
        b4b = sb("b4b", [NP, D])
        fold = sb("fold", [2 * D + 1, D + 1])
        hT = sb("hT", [P, 2, NP])

        bank = [ctx.enter_context(nc.psum_tensor(f"bank{n}", [P, 512], F32)) for n in range(8)]

        x_in, dst_in, src_in, w_in = sem("x_in"), sem("dst_in"), sem("src_in"), sem("w_in")
        const = sem("const")
        pool = sem("pool")
        rel_ready = sem("rel_ready")
        dve = sem("dve")
        rmm_T, idx_T = sem("rmm_T"), sem("idx_T")
        g_out, g_in, rel_out = sem("g_out"), sem("g_in"), sem("rel_out")
        wtab_out, ptab_out, qtab_out, z_out = sem("wtab_out"), sem("ptab_out"), sem("qtab_out"), sem("z_out")
        agg_mm, x1_ready, centred, squared, var_ready, std_ready, normed, h_ready = (
            sem(n) for n in ("agg_mm", "x1_ready", "centred", "squared", "var_ready", "std_ready", "normed",
                             "h_ready"))
        w_ready, w_hi, w_lo = sem("w_ready"), sem("w_hi"), sem("w_lo")
        hT_mm, hT_ready, tab_mm, tab_hi, tab_lo = (
            sem(n) for n in ("hT_mm", "hT_ready", "tab_mm", "tab_hi", "tab_lo"))
        acc_zero, res_ready, out_mm, fin, out_s = (
            sem(n) for n in ("acc_zero", "res_ready", "out_mm", "fin", "out_s"))
        stage_out = [sem(f"stage_out{n}") for n in range(STAGES)]
        go = [sem("go0"), sem("go1")]
        done = [sem("done0"), sem("done1")]
        windows = [sem("windows0"), sem("windows1")]
        opened = [sem("opened0"), sem("opened1")]
        gathered = [ring(f"gathered_{l}_", RING) for l in range(2)]
        idx_ready, s_built, sums, added = (
            [ring(f"{n}_{l}_") for l in range(2)] for n in ("idx", "s_built", "sums", "added"))
        rel_in, pwin_in, st_built = ring("rel_in"), ring("pwin_in"), ring("st_built")
        pre1, pre2, pre3 = ring("pre1_"), ring("pre2_"), ring("pre3_")
        act1, act2, hi3, lo3 = ring("act1_"), ring("act2_"), ring("hi3_"), ring("lo3_")

        def bc(ap, n):
            return ap.unsqueeze(2).to_broadcast([ap.shape[0], ap.shape[1], n])

        def part(ap, half):
            return ap[:, half * H:half * H + H + 2]

        def chunk(c):
            return slice(c * CT, (c + 1) * CT)

        at = {}
        xd = x.rearrange("(p t) d -> p t d", t=NT)
        od = out.rearrange("(p t) d -> p t d", t=NT)
        accn = acc[:, 0:N].rearrange("f (p t) -> f t p", t=NT)
        SPLIT = NP // 16 * 16
        PARTS = [(0, SPLIT), (SPLIT, NP)]
        per = 512 // P
        NTB = -(-NBLK // per)
        last = NBLK - 1

        def nsweeps(eng):
            return eng.value_load(span_i[0:1, 0:1], min_val=1, max_val=-(-N // WIN))

        block = ctx.enter_context(nc.Block())

        @block.vector
        def _(v):
            n = [0]

            def link(ins):
                n[0] += 1
                ins.then_inc(dve, 1)

            def settle():
                v.wait_ge(dve, n[0])

            def centre(l, c):
                k = chunk(c)
                link(nc.vector.tensor_reduce(mu[:, k], xs[:, k, :], AX.X, ALU.add))
                settle()
                link(nc.vector.tensor_scalar(mu[:, k], mu[:, k], 1.0 / D, None, ALU.mult))
                settle()
                nc.vector.tensor_tensor(tmp[:, k, :], xs[:, k, :], bc(mu[:, k], D), ALU.subtract)\
                    .then_inc(centred, 1)

            def variance(l, c):
                v.wait_ge(squared, l * NC + c + 1)
                nc.vector.tensor_reduce(var[:, chunk(c)], sq[:, chunk(c), :], AX.X, ALU.add)\
                    .then_inc(var_ready, 1)

            def normalise(l, c):
                k = chunk(c)
                v.wait_ge(std_ready, l * NC + c + 1)
                link(nc.vector.reciprocal(rstd[:, k], std[:, k]))
                settle()
                nc.vector.tensor_tensor(tmp[:, k, :], tmp[:, k, :], bc(rstd[:, k], D), ALU.mult)\
                    .then_inc(normed, 1)

            def sweep_start(l, s):
                nc.vector.tensor_tensor(relT[:, :].rearrange("p (g k) -> p g k", k=SUB),
                                        dstT[:, :].rearrange("p (g k) -> p g k", k=SUB),
                                        bc(base_f[:, :], SUB), ALU.subtract).then_inc(windows[l], 1)
                nc.vector.tensor_scalar(base_i[:, :], base_f[:, :], float(N), None, ALU.min)\
                    .then_inc(windows[l], 1)
                v.wait_ge(windows[l], s * 6 + 2)
                c = E // P
                nc.vector.memset(relT[:, c + 1:NSUB], -1.0).then_inc(windows[l], 1)
                nc.vector.memset(relT[E - c * P:P, c:c + 1], -1.0).then_inc(windows[l], 1)
                v.wait_ge(windows[l], s * 6 + 4)
                v.sem_inc(go[l], 1)

            def sweep_end(l, s):
                for sm in added[l]:
                    v.wait_ge(sm, (s + 1) * (NG // DEEP))
                nc.vector.tensor_scalar(base_f[:, :], base_f[:, :], float(WIN), None, ALU.add)\
                    .then_inc(windows[l], 1)
                nc.vector.tensor_scalar(negid[:, :], negid[:, :], float(-WIN), None, ALU.add)\
                    .then_inc(windows[l], 1)
                v.wait_ge(windows[l], s * 6 + 6)

            def copy_index(l, i, u):
                if i.valid(u, -LEAD):
                    k = slot(u, -LEAD)
                    wait_slot(v, gathered[l], i, u, RING - LEAD, 16 * SUB)
                    g = i.group + u + LEAD
                    nc.vector.tensor_copy(idx[:, k, :], srcT[:, bass.ds(g * SUB, SUB)])\
                        .then_inc(idx_ready[l][k % DEEP], 1)

            def build_S(l, i, u):
                if i.valid(u, 0):
                    wait_slot(v, sums[l], i, u, DEEP)
                    g = i.group + u
                    nc.vector.tensor_tensor(
                        S[:, u % DEEP, :, :], iota_f[:, :].unsqueeze(1).to_broadcast([P, SUB, WIN]),
                        bc(relT[:, bass.ds(g * SUB, SUB)], WIN), ALU.is_equal).then_inc(s_built[l][u % DEEP], 1)

            def add_sums(l, rows, banks, i, u, lag):
                if not i.valid(u, lag):
                    return
                base = v.value_load(base_i[0:1, bass.ds(i.group + u - lag, 1)], min_val=0, max_val=N)
                wait_slot(v, sums[l], i, u, lag)
                wait_slot(v, added[l], i, u, lag + 1)
                s = slot(u, lag)
                nc.vector.tensor_tensor(acc[0:rows, bass.ds(base, WIN)], acc[0:rows, bass.ds(base, WIN)],
                                        banks[s % 2][0:rows, 0:WIN], ALU.add).then_inc(added[l][s % DEEP], 1)

            v.wait_ge(const, 2)
            link(nc.vector.tensor_copy(iota_f[:, :], iota_i[:, :]))
            link(nc.vector.tensor_copy(negid[:, :], negid_i[:, :]))
            link(nc.vector.memset(epsc[:, :], EPS))
            link(nc.vector.memset(rmm[:, :, :], 0.0))
            link(nc.vector.memset(zrow[:, :], 0.0))
            at["zeros"] = n[0]
            settle()
            v.wait_ge(dst_in, 16 * 5)
            link(nc.vector.tensor_copy(dst_r[:, 0:last, :], dst_i[:, 0:last, :]))
            link(nc.vector.tensor_copy(dst_r[0:LASTQ, last, :], dst_i[0:LASTQ, last, :]))
            at["dst_r"] = n[0]
            settle()
            for m, op in enumerate((ALU.min, ALU.max)):
                link(nc.vector.tensor_reduce(rmm[:, m, 0:last], dst_r[:, 0:last, :], AX.X, op))
                link(nc.vector.tensor_reduce(rmm[0:LASTQ, m, last:NBLK], dst_r[0:LASTQ, last:NBLK, :], AX.X, op))
            at["rmm"] = n[0]
            v.wait_ge(src_in, 16 * 5)
            link(nc.vector.tensor_copy(src_r[:, 0:last, :], src_i[:, 0:last, :]))
            link(nc.vector.tensor_copy(src_r[0:LASTQ, last, :], src_i[0:LASTQ, last, :]))
            at["src_r"] = n[0]
            v.wait_ge(rmm_T, 1)
            for m, op in enumerate((ALU.min, ALU.max)):
                link(nc.vector.tensor_reduce(
                    gmm[:, m, :], bank[m][0:NBLK, 0:P].rearrange("b (g k) -> b g k", k=SUB), AX.X, op))
            at["gmm"] = n[0]
            v.wait_ge(x_in, 16 * 6)
            for c in range(NC + 3):
                if c < NC:
                    centre(0, c)
                if 0 <= c - 1 < NC:
                    variance(0, c - 1)
                if 0 <= c - 2 < NC:
                    k = chunk(c - 2)
                    normalise(0, c - 2)
                    v.wait_ge(normed, c - 1)
                    nc.vector.scalar_tensor_tensor(sq[:, k, :], tmp[:, k, :], 0.0, bc(n1[:, k], D),
                                                   ALU.max, ALU.mult).then_inc(w_ready, 1)
                if c >= 3:
                    k = chunk(c - 3)
                    v.wait_ge(w_hi, c - 2)
                    nc.vector.tensor_tensor(wst[:, k, 1, :], sq[:, k, :], wst[:, k, 0, :], ALU.subtract)\
                        .then_inc(w_lo, 1)
            v.wait_ge(g_in, 16 * 6)
            link(nc.vector.tensor_tensor(gtop[:, :], gtop[:, :], base0[:, :], ALU.subtract))
            link(nc.vector.tensor_copy(base_f[:, :], base0[:, :]))
            settle()
            link(nc.vector.tensor_reduce(span[:, :], gtop[:, :], AX.X, ALU.max))
            settle()
            link(nc.vector.tensor_copy(span_i[:, :], span[:, :]))
            settle()
            link(nc.vector.tensor_scalar(span_i[:, :], span_i[:, :], WIN.bit_length() - 1, None,
                                         ALU.arith_shift_right))
            settle()
            link(nc.vector.tensor_scalar(span_i[:, :], span_i[:, :], 1, None, ALU.add))
            settle()
            at["span"] = n[0]
            for k in range(NTB):
                a, b = k * 512, min((k + 1) * 512, NSUB)
                v.wait_ge(idx_T, 1 + k)
                link(nc.vector.tensor_copy(srcT[:, a:b], bank[2 + k % 2][:, 0:b - a]))
                at[("srcT", k)] = n[0]
            for k in range(NTB):
                a, b = k * 512, min((k + 1) * 512, NSUB)
                v.wait_ge(idx_T, 1 + NTB + k)
                link(nc.vector.tensor_copy(dstT[:, a:b], bank[2 + k % 2][:, 0:b - a]))
                at[("dstT", k)] = n[0]
            link(nc.vector.memset(ones3[:, :], 1.0))
            settle()

            def step0(i, u):
                copy_index(0, i, u)
                build_S(0, i, u)
                add_sums(0, 2 * D + 1, [bank[0], bank[1]], i, u, 2)

            v.wait_ge(acc_zero, 1)
            with v.Fori(0, nsweeps(v)) as s:
                sweep_start(0, s)
                run_steps(v, step0, LEAD, 2, s)
                sweep_end(0, s)
            v.sem_inc(done[0], 1)
            link(nc.vector.tensor_copy(base_f[:, :], base0[:, :]))
            link(nc.vector.tensor_copy(negid[:, :], negid_i[:, :]))

            v.wait_ge(w_in, 16 * 16)
            v.wait_ge(const, 5)
            for k in range(TC):
                r = slice(k * D, (k + 1) * D)
                link(nc.vector.tensor_tensor(wpq[r, k, 0:H], w1a[r, :], w1b[r, :], ALU.subtract))
                link(nc.vector.tensor_copy(wpq[r, k, H:2 * H], w1b[r, :]))
            for k in range(3):
                link(nc.vector.tensor_copy(bpart[:, k, :, :], brow[:, :, :]))
                settle()
                if k < 2:
                    link(nc.vector.tensor_tensor(brow[:, :, :], brow[:, :, :], bpart[:, k, :, :], ALU.subtract))
                    settle()
            link(nc.vector.tensor_tensor(bmask[:, :, :, :].rearrange("p k a b -> p k (a b)"),
                                         bpart[:, :, :, :].rearrange("p k a b -> p k (a b)"),
                                         bc(ident[0:3, 0:3], 2 * H), ALU.mult))
            for k in range(1, 3):
                settle()
                link(nc.vector.tensor_tensor(bmask[:, 0, :, :], bmask[:, 0, :, :], bmask[:, k, :, :], ALU.add))
            settle()
            link(nc.vector.tensor_copy(b1s[:, :, 0:H], bmask[:, 0, 0:1, :].to_broadcast([3, TC, H])))
            link(nc.vector.tensor_copy(b3s[:, :, :], bmask[:, 0, 1:2, :].to_broadcast([3, SUB, H])))
            at["weights"] = n[0]

            v.wait_ge(wtab_out, 16 * 2 * NC)
            link(nc.vector.memset(qrow[:, :, :, 2 * H:RW].bitcast(F32), 0.0))
            link(nc.vector.memset(pwin[:, :, 2 * H:RW].bitcast(F32), 0.0))

            def gain(c):
                for b in range(2):
                    m = 2 * c + b
                    k = slice(m * CT // 2, (m + 1) * CT // 2)
                    o = bank[m % 2][0:NP, 0:CT // 2 * (D + 1)].rearrange("p (t d) -> p t d", d=D + 1)
                    v.wait_ge(agg_mm, m + 1)
                    link(nc.vector.tensor_tensor(tmp[:, k, :], o[:, :, 0:D], bc(n2[:, k], D), ALU.mult))
                    link(nc.vector.tensor_copy(deg[:, k], o[:, :, D]))
                    at[("agg", m)] = n[0]
                settle()
                link(nc.vector.tensor_tensor(xs[:, chunk(c), :], xs[:, chunk(c), :], tmp[:, chunk(c), :], ALU.add))
                settle()

            def tables_lo(c):
                for m in range(CT // TC * c, CT // TC * (c + 1)):
                    o = bank[4 + m % 4][0:NP, :].rearrange("p (t c h) -> p t c h", t=TC, c=2)
                    v.wait_ge(tab_hi, m + 1)
                    nc.vector.tensor_tensor(stage[:, m % STAGES, :, 1::2, :], o,
                                            stage[:, m % STAGES, :, 0::2, :], ALU.subtract).then_inc(tab_lo, 1)

            for c in range(NC + 3):
                if c < NC:
                    gain(c)
                    centre(1, c)
                if 0 <= c - 1 < NC:
                    variance(1, c - 1)
                if 0 <= c - 2 < NC:
                    normalise(1, c - 2)
                if c >= 3:
                    tables_lo(c - 3)
            link(nc.vector.tensor_scalar(rdeg[:, :], deg[:, :], 1.0, None, ALU.max))
            link(nc.vector.tensor_scalar(has[:, :], deg[:, :], 1.0, None, ALU.min))
            settle()
            link(nc.vector.reciprocal(rdeg[:, :], rdeg[:, :]))
            link(nc.vector.tensor_tensor(tmp[:, :, :], b4b[:, :].unsqueeze(1).to_broadcast([NP, NT, D]),
                                         bc(has[:, :], D), ALU.mult))
            settle()
            link(nc.vector.tensor_tensor(xs[:, :, :], xs[:, :, :], tmp[:, :, :], ALU.add))

            def build_ST(i, u):
                if i.valid(u, -1):
                    s = slot(u, -1)
                    wait_slot(v, rel_in, i, u, -1, 16)
                    wait_slot(v, pre1, i, u, DEEP - 1)
                    nc.vector.tensor_scalar(ST[:, s % DEEP, :], relb[:, s % DEEP, :], negid[:, 0:1], None, ALU.is_equal)\
                        .then_inc(st_built[s % DEEP], 1)

            def step1(i, u):
                copy_index(1, i, u)
                if i.valid(u, 3):
                    s = slot(u, 3)
                    wait_slot(v, hi3, i, u, 3)
                    nc.vector.scalar_tensor_tensor(
                        h3[:, s % 2, :, H:2 * H], bank[4 + s % 2][:, 0:SUB * H].rearrange("p (k f) -> p k f", f=H),
                        0.0, h3[:, s % 2, :, 0:H], ALU.max, ALU.subtract).then_inc(lo3[s % DEEP], 1)
                add_sums(1, P, [bank[6], bank[7]], i, u, 4)
                build_ST(i, u)
                build_S(1, i, u)

            v.wait_ge(acc_zero, 2)
            with v.Fori(0, nsweeps(v)) as s:
                sweep_start(1, s)
                run_steps(v, step1, LEAD, 4, s)
                sweep_end(1, s)
            v.sem_inc(done[1], 1)

            for m in range(NOUT):
                k = slice(m * OT, min((m + 1) * OT, NT))
                w = k.stop - k.start
                v.wait_ge(out_mm, m + 1)
                link(nc.vector.tensor_tensor(tmp[:, k, :],
                                             bank[m][0:NP, 0:w * D].rearrange("p (t d) -> p t d", d=D),
                                             bc(rdeg[:, k], D), ALU.mult))
                settle()
                nc.vector.tensor_tensor(sq[:, k, :], tmp[:, k, :], xs[:, k, :], ALU.add).then_inc(fin, 1)

        @block.tensor
        def _(t):
            t.wait_ge(const, 3)
            t.wait_ge(dve, at["rmm"])
            for m in range(2):
                ins = nc.tensor.transpose(bank[m][0:NBLK, 0:P], rmm[:, m, :], ident[:, :])
            ins.then_inc(rmm_T, 1)
            for which, rows, other in (("srcT", src_r, None), ("dstT", dst_r, "srcT")):
                t.wait_ge(dve, at["src_r"])
                for k in range(NTB):
                    prev = (which, k - 2) if k >= 2 else ((other, NTB - 2 + k) if other else None)
                    if prev:
                        t.wait_ge(dve, at[prev])
                    for b in range(k * per, min((k + 1) * per, NBLK)):
                        q = P if b < last else LASTQ
                        c = (b - k * per) * P
                        ins = nc.tensor.transpose(bank[2 + k % 2][:, c:c + q], rows[0:q, b, :], ident[0:q, 0:q])
                    ins.then_inc(idx_T, 1)

            def step0(i, u):
                if not i.valid(u, 0):
                    return
                wait_slot(t, s_built[0], i, u, 0)
                wait_slot(t, gathered[0], i, u, 0, 16 * SUB)
                wait_slot(t, added[0], i, u, 2)
                for k in range(SUB):
                    ins = nc.tensor.matmul(bank[u % 2][0:2 * D + 2, 0:WIN], wrow[:, u, k, :], S[:, u % DEEP, k, :],
                                           start=(k == 0), stop=(k == SUB - 1))
                ins.then_inc(sums[0][u % DEEP], 1)

            with t.Fori(0, nsweeps(t)) as s:
                t.wait_ge(go[0], s + 1)
                run_steps(t, step0, 0, 0, s)
            t.wait_ge(done[0], 1)

            def aggregate(c):
                for m in range(2 * c, 2 * c + 2):
                    if m >= 2:
                        t.wait_ge(dve, at[("agg", m - 2)])
                    for j in range(CT // 2):
                        ins = nc.tensor.matmul(bank[m % 2][0:NP, j * (D + 1):(j + 1) * (D + 1)],
                                               accn[0:2 * D + 1, m * CT // 2 + j, :], fold[:, :],
                                               start=True, stop=True)
                    ins.then_inc(agg_mm, 1)

            def tables(c):
                lo, hi = CT // TC * c, CT // TC * (c + 1)
                t.wait_ge(h_ready, c + 1)
                for m in range(lo, hi + 1):
                    if m < hi:
                        if m >= 2:
                            t.wait_ge(hT_ready, m - 1)
                        nc.tensor.transpose(bank[2 + m % 2][:, 0:NP],
                                            sq[:, TC * m:TC * (m + 1), :].rearrange("p a b -> p (a b)"),
                                            ident[0:NP, 0:NP]).then_inc(hT_mm, 1)
                    j = m - 1
                    if j >= lo:
                        t.wait_ge(hT_ready, j + 1)
                        if j >= 4:
                            t.wait_ge(tab_lo, j - 3)
                        o = bank[4 + j % 4][0:NP, :]
                        nc.tensor.matmul(o, ones3[:, 0:NP], b1s[:, :, :].rearrange("p a b -> p (a b)"),
                                         start=True, stop=False)
                        nc.tensor.matmul(o, hT[:, j % 2, :], wpq[:, :, :].rearrange("p a b -> p (a b)"),
                                         start=False, stop=True).then_inc(tab_mm, 1)

            t.wait_ge(dve, at["weights"])
            for c in range(NC + 3):
                if c < NC:
                    aggregate(c)
                if c >= 3:
                    tables(c - 3)

            def step1(i, u):
                if i.valid(u, 0):
                    wait_slot(t, act1, i, u, 2)
                    wait_slot(t, st_built, i, u, 0)
                    wait_slot(t, pwin_in, i, u, 0, 16)
                    for half in range(2):
                        nc.tensor.matmul(bank[u % 2][0:H + 2, :], part(pwin[:, u % DEEP, :], half), ST[:, u % DEEP, :],
                                         start=(half == 0), stop=False)
                    wait_slot(t, gathered[1], i, u, 0, 16 * SUB)
                    for k in range(SUB):
                        for half in range(2):
                            ins = nc.tensor.matmul(bank[u % 2][0:H + 2, k * P:(k + 1) * P],
                                                   part(qrow[:, u, k, :], half), identr[:, :],
                                                   start=False, stop=(k == SUB - 1 and half == 1))
                    ins.then_inc(pre1[u % DEEP], 1)
                if i.valid(u, 1):
                    s = slot(u, 1)
                    wait_slot(t, act1, i, u, 1)
                    wait_slot(t, act2, i, u, 3)
                    nc.tensor.matmul(bank[2 + s % 2][:, :], w2s[:, :], h1[:, s % 2, :], start=True, stop=True)\
                        .then_inc(pre2[s % DEEP], 1)
                if i.valid(u, 2):
                    s = slot(u, 2)
                    wait_slot(t, act2, i, u, 2)
                    wait_slot(t, lo3, i, u, 4)
                    nc.tensor.matmul(bank[4 + s % 2][:, 0:SUB * H], ones3[:, :],
                                     b3s[:, :, :].rearrange("p a b -> p (a b)"), start=True, stop=False)
                    for k in range(SUB):
                        ins = nc.tensor.matmul(bank[4 + s % 2][:, k * H:(k + 1) * H],
                                               h2[:, s % 2, k * P:(k + 1) * P], w3s[:, :],
                                               start=False, stop=(k == SUB - 1))
                    ins.then_inc(pre3[s % DEEP], 1)
                if i.valid(u, 3):
                    s = slot(u, 3)
                    wait_slot(t, lo3, i, u, 3)
                    wait_slot(t, s_built[1], i, u, 3)
                    wait_slot(t, added[1], i, u, 5)
                    for k in range(SUB):
                        ins = nc.tensor.matmul(bank[6 + s % 2][:, 0:WIN], h3[:, s % 2, k, :], S[:, s % DEEP, k, :],
                                               start=(k == 0), stop=(k == SUB - 1))
                    ins.then_inc(sums[1][s % DEEP], 1)

            with t.Fori(0, nsweeps(t)) as s:
                t.wait_ge(go[1], s + 1)
                run_steps(t, step1, 0, 3, s)
            t.wait_ge(done[1], 1)

            for m in range(NOUT):
                for c in range(m * OT, min((m + 1) * OT, NT)):
                    ins = nc.tensor.matmul(bank[m][0:NP, (c - m * OT) * D:(c - m * OT + 1) * D],
                                           accn[:, c, :], w4s[:, :], start=True, stop=True)
                ins.then_inc(out_mm, 1)

        @block.scalar
        def _(a):
            def square(l, c):
                a.wait_ge(centred, l * NC + c + 1)
                nc.scalar.activation(sq[:, chunk(c), :], tmp[:, chunk(c), :], ACT.Square).then_inc(squared, 1)

            def root(l, c):
                a.wait_ge(var_ready, l * NC + c + 1)
                nc.scalar.activation(std[:, chunk(c)], var[:, chunk(c)], ACT.Sqrt, bias=epsc[0:NP, :],
                                     scale=1.0 / D).then_inc(std_ready, 1)

            for k in range(TC):
                a.dma_start(w1a[k * D:(k + 1) * D, :], W1[0:D, :]).then_inc(w_in, 16)
                a.dma_start(w1b[k * D:(k + 1) * D, :], W1[D:2 * D, :]).then_inc(w_in, 16)
            a.dma_start(w2s[:, :], W2).then_inc(w_in, 16)
            for k in range(2):
                a.dma_start(w4s[k * H:(k + 1) * H, :], W4).then_inc(w_in, 16)
            a.dma_start(b2c[:, :], b2.unsqueeze(1)).then_inc(w_in, 16)
            a.dma_start(w3s[:, :], W3).then_inc(w_in, 16)
            a.dma_start(brow[:, 0, :], b1.unsqueeze(0).to_broadcast([3, H])).then_inc(w_in, 16)
            a.dma_start(brow[:, 1, :], b3.unsqueeze(0).to_broadcast([3, H])).then_inc(w_in, 16)
            a.dma_start(b4b[:, :], b4.unsqueeze(0).to_broadcast([NP, D])).then_inc(w_in, 16)
            for c in range(NC + 2):
                if c < NC:
                    square(0, c)
                if 0 <= c - 1 < NC:
                    root(0, c - 1)
                if c >= 2:
                    a.wait_ge(w_ready, c - 1)
                    nc.scalar.activation(wst[:, chunk(c - 2), 0, :], sq[:, chunk(c - 2), :], ACT.Copy)\
                        .then_inc(w_hi, 1)

            a.wait_ge(g_in, 16 * 6)
            for b in range(NBLK):
                q = P if b < last else LASTQ
                nc.scalar.activation(rel_r[0:q, b, :], dst_r[0:q, b, :], ACT.Identity,
                                     bias=base_row[0:q, b:b + 1], scale=-1.0).then_inc(rel_ready, 1)

            def tables_hi(c):
                for m in range(CT // TC * c, CT // TC * (c + 1) + 1):
                    if m < CT // TC * (c + 1):
                        a.wait_ge(hT_mm, m + 1)
                        if m >= 2:
                            a.wait_ge(tab_mm, m - 1)
                        nc.scalar.activation(hT[:, m % 2, :], bank[2 + m % 2][:, 0:NP], ACT.Copy)\
                            .then_inc(hT_ready, 1)
                    j = m - 1
                    if j >= CT // TC * c:
                        a.wait_ge(tab_mm, j + 1)
                        if j >= STAGES:
                            a.wait_ge(stage_out[j % STAGES], j // STAGES * 64)
                        nc.scalar.activation(stage[:, j % STAGES, :, 0::2, :],
                                             bank[4 + j % 4][0:NP, :].rearrange("p (t c h) -> p t c h", t=TC, c=2),
                                             ACT.Copy).then_inc(tab_hi, 1)

            a.wait_ge(rel_out, 32)
            for c in range(NC + 3):
                if c < NC:
                    square(1, c)
                if 0 <= c - 1 < NC:
                    root(1, c - 1)
                if 0 <= c - 2 < NC:
                    a.wait_ge(normed, NC + c - 1)
                    nc.scalar.activation(sq[:, chunk(c - 2), :], tmp[:, chunk(c - 2), :], ACT.Relu)\
                        .then_inc(h_ready, 1)
                if c >= 3:
                    tables_hi(c - 3)

            def step1(i, u):
                if i.valid(u, 0):
                    wait_slot(a, pre1, i, u, 0)
                    wait_slot(a, pre2, i, u, 2)
                    nc.scalar.activation(h1[:, u % 2, :], bank[u % 2][0:H, :], ACT.Relu).then_inc(act1[u % DEEP], 1)
                if i.valid(u, 1):
                    s = slot(u, 1)
                    wait_slot(a, pre2, i, u, 1)
                    wait_slot(a, pre3, i, u, 3)
                    nc.scalar.activation(h2[:, s % 2, :], bank[2 + s % 2][:, :], ACT.Relu, bias=b2c[:, 0:1])\
                        .then_inc(act2[s % DEEP], 1)
                if i.valid(u, 2):
                    s = slot(u, 2)
                    wait_slot(a, pre3, i, u, 2)
                    wait_slot(a, sums[1], i, u, 4)
                    nc.scalar.activation(h3[:, s % 2, :, 0:H],
                                         bank[4 + s % 2][:, 0:SUB * H].rearrange("p (k f) -> p k f", f=H),
                                         ACT.Relu).then_inc(hi3[s % DEEP], 1)

            with a.Fori(0, nsweeps(a)) as s:
                a.wait_ge(go[1], s + 1)
                run_steps(a, step1, 0, 2, s)

        @block.gpsimd
        def _(g):
            n = [0]

            def link(ins):
                n[0] += 1
                ins.then_inc(pool, 1)

            def settle():
                g.wait_ge(pool, n[0])

            nc.gpsimd.iota(iota_i[:, :], pattern=[[1, P]], base=0, channel_multiplier=0).then_inc(const, 1)
            nc.gpsimd.iota(negid_i[:, :], pattern=[[0, 1]], base=0, channel_multiplier=-1).then_inc(const, 1)
            link(nc.gpsimd.memset(ident[:, :], 0.0))
            settle()
            link(nc.gpsimd.affine_select(out=ident[:, :], in_=ident[:, :], compare_op=ALU.not_equal, fill=1.0,
                                         base=0, pattern=[[-1, P]], channel_multiplier=1))
            settle()
            nc.gpsimd.tensor_copy(identr[:, :], ident[:, :]).then_inc(const, 1)
            link(nc.gpsimd.memset(fold[:, :], 0.0))
            link(nc.gpsimd.memset(wrow[:, :, :, 2 * D + 1:2 * D + 2].bitcast(F32), 0.0))
            link(nc.gpsimd.memset(wrow[:, :, :, 2 * D:2 * D + 1].bitcast(F32), 1.0))
            settle()
            link(nc.gpsimd.tensor_copy(fold[0:D, 0:D], ident[0:D, 0:D]))
            link(nc.gpsimd.tensor_copy(fold[D:2 * D, 0:D], ident[D:2 * D, D:2 * D]))
            link(nc.gpsimd.memset(fold[2 * D:2 * D + 1, D:D + 1], 1.0))
            settle()
            nc.gpsimd.memset(acc[0:2 * D + 1, :], 0.0).then_inc(acc_zero, 1)
            nc.gpsimd.memset(wpq[:, :, :], 0.0).then_inc(const, 1)
            nc.gpsimd.memset(b1s[:, :, :], 0.0).then_inc(const, 1)

            def gathers(l, table, rows, width, stored, total):
                def step(i, u):
                    wait_slot(g, idx_ready[l], i, u, 0)
                    free = sums[0] if l == 0 else pre1
                    wait_slot(g, free, i, u, RING)
                    g.sem_inc(opened[l], 1)
                    g.wait_ge(stored, total)
                    for k in range(SUB):
                        nc.gpsimd.indirect_dma_start(
                            out=rows[:, u, k, 0:width].bitcast(F32), out_offset=None, in_=table,
                            in_offset=bass.IndirectOffsetOnAxis(ap=idx[:, u, k:k + 1], axis=0))\
                            .then_inc(gathered[l][u], 16)
                return step

            g.wait_ge(dve, at["span"])
            with g.Fori(0, nsweeps(g)) as s:
                g.wait_ge(go[0], s + 1)
                run_steps(g, gathers(0, wtab, wrow, 2 * D, wtab_out, 16 * 2 * NC), 0, 0, s)

            g.wait_ge(agg_mm, 2 * NC)
            nc.gpsimd.memset(acc[:, :], 0.0).then_inc(acc_zero, 1)
            for sm in stage_out:
                g.wait_ge(sm, NT // TC // STAGES * 64)
            with g.Fori(0, nsweeps(g)) as s:
                g.wait_ge(go[1], s + 1)
                run_steps(g, gathers(1, qtab, qrow, 2 * H, stage_out[0], NT // TC // STAGES * 64), 0, 0, s)

        @block.sync
        def _(y):
            full = last * P * P
            mid = full + REALQ * P
            for ids, tile_, landed in ((dst, dst_i, dst_in), (src, src_i, src_in)):
                y.dma_start(tile_[:, 0:last, :], ids[0:full].rearrange("(b q e) -> q b e", q=P, e=P))\
                    .then_inc(landed, 16)
                y.dma_start(tile_[0:REALQ, last, :], ids[full:mid].rearrange("(q e) -> q e", e=P))\
                    .then_inc(landed, 16)
                y.dma_start(tile_[REALQ:REALQ + 1, last, 0:REALR], ids[mid:E].unsqueeze(0)).then_inc(landed, 16)
                y.dma_start(tile_[REALQ:REALQ + 1, last, REALR:P], ids[E - (P - REALR):E].unsqueeze(0))\
                    .then_inc(landed, 16)
                k = LASTQ - REALQ - 1
                y.dma_start(tile_[REALQ + 1:LASTQ, last, :],
                            ids[E - k * P:E].rearrange("(q e) -> q e", e=P)).then_inc(landed, 16)
            for a, b in PARTS:
                y.dma_start(xs[a:b, :, :], xd[a:b, :, :]).then_inc(x_in, 16)
                y.dma_start(n1[a:b, :], nv1.rearrange("(p t) o -> p (t o)", t=NT)[a:b, :]).then_inc(x_in, 16)
                y.dma_start(n2[a:b, :], nv2.rearrange("(p t) o -> p (t o)", t=NT)[a:b, :]).then_inc(x_in, 16)
            y.wait_ge(dve, at["gmm"])
            y.dma_start(gmin_d.rearrange("(b g) -> b g", g=GB), gmm[:, 0, :]).then_inc(g_out, 16)
            y.dma_start(gmax_d.rearrange("(b g) -> b g", g=GB), gmm[:, 1, :]).then_inc(g_out, 16)
            y.wait_ge(g_out, 32)
            y.dma_start(base0[:, :], gmin_d[0:NG].unsqueeze(0).to_broadcast([P, NG])).then_inc(g_in, 16)
            y.dma_start(gtop[:, :], gmax_d[0:NG].unsqueeze(0).to_broadcast([P, NG])).then_inc(g_in, 16)
            for r in range(SUB):
                y.dma_start(base_row[r:P:SUB, :], gmin_d.rearrange("(b g) -> g b", g=GB),
                            allow_slow_non_contiguous=True).then_inc(g_in, 16)
            wd = wtab.rearrange("(p t) (c d) -> p t c d", t=NT, c=2)
            for c in range(NC):
                y.wait_ge(w_lo, c + 1)
                for a, b in PARTS:
                    y.dma_start(wd[a:b, chunk(c), :, :], wst[a:b, chunk(c), :, :].bitcast(F32)).then_inc(wtab_out, 16)
            y.dma_start(ptab[N:N + WIN, :], zrow[:, :]).then_inc(z_out, 16)
            y.wait_ge(rel_ready, NBLK)
            y.dma_start(rel_d[0:last * P, :].rearrange("(b q) e -> q b e", q=P), rel_r[:, 0:last, :])\
                .then_inc(rel_out, 16)
            y.dma_start(rel_d[last * P:NSUB, :], rel_r[0:LASTQ, last, :]).then_inc(rel_out, 16)
            pd = ptab[0:N, :].rearrange("(p t) (c h) -> p t c h", t=NT, c=2)
            qd = qtab.rearrange("(p t) (c h) -> p t c h", t=NT, c=2)
            for m in range(NT // TC):
                y.wait_ge(tab_lo, m + 1)
                for a, b in PARTS:
                    for c, table in ((0, pd), (2, qd)):
                        y.dma_start(table[a:b, TC * m:TC * (m + 1), :, :], stage[a:b, m % STAGES, :, c:c + 2, :].bitcast(F32))\
                            .then_inc(stage_out[m % STAGES], 16)
            y.wait_ge(z_out, 16)
            y.wait_ge(rel_out, 32)
            for sm in stage_out:
                y.wait_ge(sm, NT // TC // STAGES * 64)

            relg = rel_d.rearrange("(g k) e -> g (k e)", k=SUB)

            def step1(i, u):
                g = i.group + u
                wait_slot(y, st_built, i, u, DEEP)
                y.dma_start(relb[:, u % DEEP, :], relg[bass.ds(g, 1), :].to_broadcast([P, GE]))\
                    .then_inc(rel_in[u % DEEP], 16)
                base = y.value_load(base_i[0:1, bass.ds(g, 1)], min_val=0, max_val=N)
                wait_slot(y, pre1, i, u, DEEP)
                y.dma_start(pwin[:, u % DEEP, 0:2 * H].bitcast(F32), ptab[bass.ds(base, WIN), :]).then_inc(pwin_in[u % DEEP], 16)

            with y.Fori(0, nsweeps(y)) as s:
                y.wait_ge(go[1], s + 1)
                run_steps(y, step1, 0, 0, s)

            y.wait_ge(fin, NOUT)
            for a, b in PARTS:
                y.dma_start(od[a:b, :, :], sq[a:b, :, :]).then_inc(out_s, 16)
            y.wait_ge(out_s, 32)


_INS = ["x", "src", "dst", "node_vec1", "node_vec1_n2", "L1_gnn_W1", "L1_gnn_b1", "L1_gnn_W2", "L1_gnn_b2",
        "L1_gnn_W3", "L1_gnn_b3", "L1_gnn_W4", "L1_gnn_b4"]


def kernel(**inputs):
    import numpy as _np
    import concourse.bacc as _bacc
    from concourse import mybir as _mybir
    from concourse.bass_utils import run_bass_kernel_spmd as _run

    nc = _bacc.Bacc("TRN2", target_bir_lowering=False, num_devices=1)
    arrays, args = {}, []
    for name in _INS:
        a = _np.ascontiguousarray(inputs[name])
        arrays[f"in_{name}_dram"] = a
        args.append(nc.dram_tensor(f"in_{name}_dram", a.shape, _mybir.dt.from_np(a.dtype), kind="ExternalInput").ap())
    args.append(nc.dram_tensor("out_dram", (N, D), _mybir.dt.float32, kind="ExternalOutput").ap())
    build(nc, *args)
    r = _run(nc, [arrays], core_ids=[0])
    return r.results[0]["out_dram"]
```

```python
from contextlib import ExitStack

import concourse.bass as bass
from concourse import mybir

ALU = mybir.AluOpType
ACT = mybir.ActivationFunctionType
AX = mybir.AxisListType
F32 = mybir.dt.float32
BF16 = mybir.dt.bfloat16
I32 = mybir.dt.int32
I16 = mybir.dt.int16
F32R = mybir.dt.float32r

P = 128
N = 12500
E = 200000
D = 32
H = 64
H2 = 2 * H
NP = 125
NT = N // NP
WIN = P
SUB = 4
GE = SUB * P
RING = 8
DEEP = 4
LEAD = 7
NG = -(-E // (GE * RING)) * RING
NIT = NG // RING
NSUB = NG * SUB
REALSUB = -(-E // P)
NBLK = -(-NSUB // P)
LASTQ = NSUB - (NBLK - 1) * P
REALQ = (E - (NBLK - 1) * P * P) // P
REALR = E - (NBLK - 1) * P * P - REALQ * P
GB = P // SUB
EPS = 1e-5
CUTS = [0, 8, 24, 44, 64, 84, NT]
NC = len(CUTS) - 1
CT = max(b - a for a, b in zip(CUTS, CUTS[1:]))
TC = 512 // (2 * H)
STAGES = 2
PW = 2
WINDOWS_AT = 4
HTS = 4
QUADS = P // D
OT = QUADS * (512 // P)
NOUT = -(-NT // OT)


def slot(u, lag):
    return (u - lag) % RING


class Turn:

    def __init__(self, number, i, sweep):
        self.number = number
        self.sweep = sweep
        self.i = i
        self.group = i * RING
        self.before = sweep * NIT + i

    def valid(self, u, lag):
        return self.number is None or 0 <= RING * self.number + u - lag < NG


def run_steps(eng, step, head, tail, sweep):
    for u in range(RING - head, RING):
        step(Turn(-1, -1, sweep), u)
    for u in range(RING):
        step(Turn(0, 0, sweep), u)
    with eng.Fori(1, NIT - 1) as i:
        for u in range(RING):
            step(Turn(None, i, sweep), u)
    for u in range(RING):
        step(Turn(NIT - 1, NIT - 1, sweep), u)
    for u in range(tail):
        step(Turn(NIT, NIT, sweep), u)


def wait_slot(eng, sems, i, u, lag, unit=1):
    r = len(sems)
    c = (u - lag) // r + 1
    if i.number is not None and i.number * (RING // r) + c <= 0:
        return
    eng.wait_ge(sems[(u - lag) % r], (i.before * (RING // r) + c) * unit)


def real_subtiles(i, u):
    return SUB if i.number != NIT - 1 else min(max(REALSUB - (i.number * RING + u) * SUB, 0), SUB)


def wait_rows(eng, gathered, i, u, lag):
    c = (u - lag) // RING
    if i.number is not None and i.number + c < 0:
        return
    s = slot(u, lag)
    missing = SUB - real_subtiles(Turn(NIT - 1, NIT - 1, 0), s)
    this = missing if i.number is not None and i.number + c == NIT - 1 else 0
    eng.wait_ge(gathered[s], i.sweep * (NIT * 16 * SUB - 16 * missing) + i.i * 16 * SUB
                + ((c + 1) * 16 * SUB - this * 16))


def build(nc, x, src, dst, nv1, nv2, W1, b1, W2, b2, W3, b3, W4, b4, out):
    ctx = ExitStack()
    with ctx:
        def sb(name, shape, dt=F32):
            return ctx.enter_context(nc.sbuf_tensor(name, shape, dt))

        def sem(name):
            return ctx.enter_context(nc.semaphore(name))

        def ring(name, n=DEEP):
            return [sem(f"{name}{u}") for u in range(n)]

        wtab = nc.dram_tensor("wtab", [N, 2 * D], F32).ap()
        qtab = nc.dram_tensor("qtab", [N, H], F32).ap()
        ptab = nc.dram_tensor("ptab", [N + WIN, H], F32).ap()
        gmin_d = nc.dram_tensor("gmin_d", [NBLK * GB], F32).ap()
        gmax_d = nc.dram_tensor("gmax_d", [NBLK * GB], F32).ap()
        rel_d = nc.dram_tensor("rel_d", [NSUB, P], I16).ap()

        xs = sb("xs", [NP, NT, D])
        tmp = sb("tmp", [NP, NT, D])
        sq = sb("sq", [NP, NT, D])
        n1 = sb("n1", [NP, NT])
        n2 = sb("n2", [NP, NT])
        mu = sb("mu", [NP, NT])
        var = sb("var", [NP, NT])
        std = sb("std", [NP, NT])
        rstd = sb("rstd", [NP, NT])
        deg = sb("deg", [NP, NT])
        rdeg = sb("rdeg", [NP, NT])
        has = sb("has", [NP, NT])
        epsc = sb("epsc", [P, 1])
        acc = sb("acc", [P, N + WIN])
        ident = sb("ident", [P, P])
        identr = sb("identr", [P, P], F32R)
        iota_i = sb("iota_i", [P, P], I32)
        iota_f = sb("iota_f", [P, P])
        negid_i = sb("negid_i", [P, 1], I32)
        negid = sb("negid", [P, 1])
        zrow = sb("zrow", [P, H])
        ones3 = sb("ones3", [3, P], BF16)
        dstT = sb("dstT", [P, NSUB])
        srcT = sb("srcT", [P, NSUB], I32)
        relT = sb("relT", [P, NSUB])
        rmm = sb("rmm", [P, 2, NBLK])
        gmm = sb("gmm", [NBLK, 2, GB])
        base0 = sb("base0", [P, NG])
        gtop = sb("gtop", [P, NG])
        base_f = sb("base_f", [P, NG])
        base_i = sb("base_i", [P, NG], I32)
        base_row = sb("base_row", [P, NBLK])
        span = sb("span", [P, 1])
        span_i = sb("span_i", [P, 1], I32)
        idx = sb("idx", [P, RING, SUB], I32)
        BW = NBLK * P
        raw = sb("raw", [P, max(2 * BW + BW // 2, STAGES * 2 * CT * H)])
        dst_r, src_r = (raw[:, k * BW:(k + 1) * BW].rearrange("p (b e) -> p b e", e=P) for k in range(2))
        dst_i, src_i = (r.bitcast(I32) for r in (dst_r, src_r))
        rel_r = raw[:, 2 * BW:2 * BW + BW // 2].bitcast(I16).rearrange("p (b e) -> p b e", e=P)
        stage = raw[0:NP, 0:STAGES * 2 * CT * H].rearrange("p (s c t h) -> p s c t h", s=STAGES, c=2, t=CT)
        WW = 2 * D + 2
        wrow = sb("wrow", [P, RING, SUB, D + WW], F32R)
        S = sb("S", [P, DEEP, SUB, WIN], F32R)
        relb = sb("relb", [P, DEEP, GE], I16)
        RW = 2 * H + 2
        sizes = [2 * SUB * RW, DEEP * GE, 2 * RW, 2 * SUB * 2 * H]
        starts = [sum(sizes[:k]) for k in range(len(sizes) + 1)]
        l1buf = sb("l1buf", [P, max(starts[-1], NT * 2 * D)], F32R)
        qsplit, ST, psplit, h3 = (l1buf[:, a:b] for a, b in zip(starts, starts[1:]))
        qsplit = qsplit.rearrange("p (r k c) -> p r k c", r=2, k=SUB)
        ST = ST.rearrange("p (r e) -> p r e", r=DEEP)
        psplit = psplit.rearrange("p (r c) -> p r c", r=2)
        h3 = h3.rearrange("p (r k c) -> p r k c", r=2, k=SUB)
        split = l1buf[0:NP, 0:NT * 2 * D].rearrange("p (t c d) -> p t c d", t=NT, c=2)
        assert H <= D + WW
        qrow = wrow[:, :, :, 0:H].bitcast(F32)
        pwin = sb("pwin", [P, DEEP, H])
        h1 = sb("h1", [H, 2, GE])
        h2 = sb("h2", [H2, 2, GE])
        w1a = sb("w1a", [P, H])
        w1b = sb("w1b", [P, H])
        wpq = sb("wpq", [P, PW, 2 * H])
        wpq_hi = sb("wpq_hi", [P, PW, 2 * H], F32R)
        wpq_lo = sb("wpq_lo", [P, PW, 2 * H], F32R)
        b1c = sb("b1c", [H, 1])
        w2s = sb("w2s", [H, H2])
        b2c = sb("b2c", [H2, 1])
        w3s = sb("w3s", [H2, H])
        brow = sb("brow", [3, H])
        bpart = sb("bpart", [3, 3, H], BF16)
        bmask = sb("bmask", [3, 3, H])
        b3s = sb("b3s", [3, SUB, H], BF16)
        w4s = sb("w4s", [P, D])
        b4b = sb("b4b", [NP, D])
        hT = sb("hT", [P, HTS, NP], F32R)

        bank = [ctx.enter_context(nc.psum_tensor(f"bank{n}", [P, 512], F32)) for n in range(8)]

        x_in, dst_in, src_in, w_in = sem("x_in"), sem("dst_in"), sem("src_in"), sem("w_in")
        const = sem("const")
        pool = sem("pool")
        rel_ready = sem("rel_ready")
        weights = sem("weights")
        dve = sem("dve")
        rmm_T, idx_T, dstT_ready = sem("rmm_T"), sem("idx_T"), sem("dstT_ready")
        g_out, g_in, rel_out = sem("g_out"), sem("g_in"), sem("rel_out")
        wtab_out, z_out = sem("wtab_out"), sem("z_out")
        agg_mm, centred, squared, var_ready, std_ready, normed, h_ready = (
            sem(n) for n in ("agg_mm", "centred", "squared", "var_ready", "std_ready", "normed", "h_ready"))
        w_hi, w_lo, h_hi = sem("w_hi"), sem("w_lo"), sem("h_hi")
        hT_mm, hT_ready, tab_mm, tab_ready = (sem(n) for n in ("hT_mm", "hT_ready", "tab_mm", "tab_ready"))
        acc_zero, out_mm, out_copied, out_T, fin, out_s = (
            sem(n) for n in ("acc_zero", "out_mm", "out_copied", "out_T", "fin", "out_s"))
        stage_out = [sem(f"stage_out{n}") for n in range(STAGES)]
        go = [sem("go0"), sem("go1")]
        done = [sem("done0"), sem("done1")]
        windows = [sem("windows0"), sem("windows1")]
        opened = [sem("opened0"), sem("opened1")]
        gathered = [ring(f"gathered_{l}_", RING) for l in range(2)]
        idx_ready, s_built, sums, added = (
            [ring(f"{n}_{l}_") for l in range(2)] for n in ("idx", "s_built", "sums", "added"))
        rel_in, pwin_in, st_built = ring("rel_in"), ring("pwin_in"), ring("st_built")
        hi1, lo1 = ring("hi1_"), ring("lo1_")
        pre1, pre2, pre3 = ring("pre1_"), ring("pre2_"), ring("pre3_")
        act1, act2, hi3, lo3 = ring("act1_"), ring("act2_"), ring("hi3_"), ring("lo3_")

        def bc(ap, n):
            return ap.unsqueeze(2).to_broadcast([ap.shape[0], ap.shape[1], n])

        def part(ap, half):
            return ap[:, half * H:half * H + H + 2]

        def chunk(c):
            return slice(CUTS[c], CUTS[c + 1])

        at = {}
        xd = x.rearrange("(p t) d -> p t d", t=NT)
        od = out.rearrange("(p t) d -> p t d", t=NT)
        accn = acc[:, 0:N].rearrange("f (p t) -> f t p", t=NT)
        NPE = NP + NP % 2
        SPLIT = NP // 16 * 16
        PARTS = [(0, SPLIT), (SPLIT, NP)]
        per = 512 // P
        NTB = -(-NBLK // per)
        last = NBLK - 1

        def stored(r):
            return len(range(r, NC, STAGES)) * 64

        def nsweeps(eng):
            return eng.value_load(span_i[0:1, 0:1], min_val=1, max_val=-(-N // WIN))

        block = ctx.enter_context(nc.Block())

        @block.vector
        def _(v):
            n = [0]

            def link(ins):
                n[0] += 1
                ins.then_inc(dve, 1)

            def settle():
                v.wait_ge(dve, n[0])

            def centre(l, c):
                k = chunk(c)
                link(nc.vector.tensor_reduce(mu[:, k], xs[:, k, :], AX.X, ALU.add))
                settle()
                nc.vector.scalar_tensor_tensor(tmp[:, k, :], bc(mu[:, k], D), -1.0 / D, xs[:, k, :],
                                               ALU.mult, ALU.add).then_inc(centred, 1)

            def variance(l, c):
                v.wait_ge(squared, l * NC + c + 1)
                nc.vector.tensor_reduce(var[:, chunk(c)], sq[:, chunk(c), :], AX.X, ALU.add)\
                    .then_inc(var_ready, 1)

            def normalise(l, c):
                k = chunk(c)
                v.wait_ge(std_ready, l * NC + c + 1)
                link(nc.vector.reciprocal(rstd[:, k], std[:, k]))
                settle()
                if l == 0:
                    link(nc.vector.tensor_tensor(rstd[:, k], rstd[:, k], n1[:, k], ALU.mult))
                    settle()
                nc.vector.scalar_tensor_tensor(sq[:, k, :], tmp[:, k, :], 0.0, bc(rstd[:, k], D),
                                               ALU.max, ALU.mult).then_inc(normed, 1)

            def sweep_start(l, s):
                nc.vector.tensor_tensor(relT[:, :].rearrange("p (g k) -> p g k", k=SUB),
                                        dstT[:, :].rearrange("p (g k) -> p g k", k=SUB),
                                        bc(base_f[:, :], SUB), ALU.subtract).then_inc(windows[l], 1)
                nc.vector.tensor_scalar(base_i[:, :], base_f[:, :], float(N), None, ALU.min)\
                    .then_inc(windows[l], 1)
                v.wait_ge(windows[l], s * 6 + 2)
                c = E // P
                nc.vector.memset(relT[:, c + 1:NSUB], -1.0).then_inc(windows[l], 1)
                nc.vector.memset(relT[E - c * P:P, c:c + 1], -1.0).then_inc(windows[l], 1)
                v.wait_ge(windows[l], s * 6 + 4)
                v.sem_inc(go[l], 1)

            def sweep_end(l, s):
                for sm in added[l]:
                    v.wait_ge(sm, (s + 1) * (NG // DEEP))
                nc.vector.tensor_scalar(base_f[:, :], base_f[:, :], float(WIN), None, ALU.add)\
                    .then_inc(windows[l], 1)
                nc.vector.tensor_scalar(negid[:, :], negid[:, :], float(-WIN), None, ALU.add)\
                    .then_inc(windows[l], 1)
                v.wait_ge(windows[l], s * 6 + 6)

            def build_S(l, i, u, lag):
                if i.valid(u, lag):
                    s = slot(u, lag) % DEEP
                    wait_slot(v, sums[l], i, u, DEEP + lag)
                    g = i.group + u - lag
                    nc.vector.tensor_tensor(
                        S[:, s, :, :], iota_f[:, :].unsqueeze(1).to_broadcast([P, SUB, WIN]),
                        bc(relT[:, bass.ds(g * SUB, SUB)], WIN), ALU.is_equal).then_inc(s_built[l][s], 1)

            def add_sums(l, rows, banks, i, u, lag):
                if not i.valid(u, lag):
                    return
                base = v.value_load(base_i[0:1, bass.ds(i.group + u - lag, 1)], min_val=0, max_val=N)
                wait_slot(v, sums[l], i, u, lag)
                wait_slot(v, added[l], i, u, lag + 1)
                s = slot(u, lag)
                nc.vector.tensor_tensor(acc[0:rows, bass.ds(base, WIN)], acc[0:rows, bass.ds(base, WIN)],
                                        banks[s % 2][0:rows, 0:WIN], ALU.add).then_inc(added[l][s % DEEP], 1)

            v.wait_ge(const, 2)
            link(nc.vector.tensor_copy(iota_f[:, :], iota_i[:, :]))
            link(nc.vector.tensor_copy(negid[:, :], negid_i[:, :]))
            link(nc.vector.memset(epsc[:, :], EPS))
            link(nc.vector.memset(rmm[:, :, :], 0.0))
            link(nc.vector.memset(zrow[:, :], 0.0))
            link(nc.vector.memset(ones3[:, :], 1.0))
            settle()
            v.wait_ge(dst_in, 16 * 5)
            link(nc.vector.tensor_copy(dst_r[:, 0:last, :], dst_i[:, 0:last, :]))
            link(nc.vector.tensor_copy(dst_r[0:LASTQ, last, :], dst_i[0:LASTQ, last, :]))
            settle()
            for m, op in enumerate((ALU.min, ALU.max)):
                link(nc.vector.tensor_reduce(rmm[:, m, 0:last], dst_r[:, 0:last, :], AX.X, op))
                link(nc.vector.tensor_reduce(rmm[0:LASTQ, m, last:NBLK], dst_r[0:LASTQ, last:NBLK, :], AX.X, op))
            at["rmm"] = n[0]
            v.wait_ge(src_in, 16 * 5)
            link(nc.vector.tensor_copy(src_r[:, 0:last, :], src_i[:, 0:last, :]))
            link(nc.vector.tensor_copy(src_r[0:LASTQ, last, :], src_i[0:LASTQ, last, :]))
            at["src_r"] = n[0]
            v.wait_ge(rmm_T, 1)
            for m, op in enumerate((ALU.min, ALU.max)):
                link(nc.vector.tensor_reduce(
                    gmm[:, m, :], bank[m][0:NBLK, 0:P].rearrange("b (g k) -> b g k", k=SUB), AX.X, op))
            at["gmm"] = n[0]
            for k in range(NTB):
                a, b = k * 512, min((k + 1) * 512, NSUB)
                v.wait_ge(idx_T, 1 + k)
                link(nc.vector.tensor_copy(srcT[:, a:b], bank[2 + k][:, 0:b - a]))
                at[("srcT", k)] = n[0]
            v.wait_ge(x_in, 16 * 6)
            for c in range(NC + 1):
                if c >= 1:
                    variance(0, c - 1)
                if c < NC:
                    centre(0, c)
                if c >= 1:
                    normalise(0, c - 1)
                if c == WINDOWS_AT:
                    v.wait_ge(g_in, 16 * 6)
                    link(nc.vector.tensor_tensor(gtop[:, :], gtop[:, :], base0[:, :], ALU.subtract))
                    link(nc.vector.tensor_copy(base_f[:, :], base0[:, :]))
                    settle()
                    link(nc.vector.tensor_reduce(span[:, :], gtop[:, :], AX.X, ALU.max))
                    settle()
                    link(nc.vector.tensor_copy(span_i[:, :], span[:, :]))
                    settle()
                    link(nc.vector.tensor_scalar(span_i[:, :], span_i[:, :], WIN.bit_length() - 1, None,
                                                 ALU.arith_shift_right))
                    settle()
                    link(nc.vector.tensor_scalar(span_i[:, :], span_i[:, :], 1, None, ALU.add))
                    settle()
                    at["span"] = n[0]

            def step0(i, u):
                build_S(0, i, u, 0)
                add_sums(0, 2 * D + 1, [bank[0], bank[1]], i, u, 2)

            v.wait_ge(acc_zero, 1)
            v.wait_ge(dstT_ready, NTB)
            with v.Fori(0, nsweeps(v)) as s:
                sweep_start(0, s)
                run_steps(v, step0, 0, 2, s)
                sweep_end(0, s)
            v.sem_inc(done[0], 1)
            link(nc.vector.tensor_copy(base_f[:, :], base0[:, :]))
            link(nc.vector.tensor_copy(negid[:, :], negid_i[:, :]))

            def gain(c):
                for m in range(CUTS[c] // TC, CUTS[c + 1] // TC):
                    k = slice(m * TC, (m + 1) * TC)
                    o = bank[m % 2][0:NP, 0:TC * (2 * D + 1)].rearrange("p (t d) -> p t d", d=2 * D + 1)
                    v.wait_ge(agg_mm, m + 1)
                    link(nc.vector.tensor_tensor(tmp[:, k, :], o[:, :, 0:D], bc(n2[:, k], D), ALU.mult))
                    link(nc.vector.tensor_copy(deg[:, k], o[:, :, 2 * D]))
                    at[("agg", m)] = n[0]
                settle()
                link(nc.vector.tensor_tensor(xs[:, chunk(c), :], xs[:, chunk(c), :], tmp[:, chunk(c), :], ALU.add))
                settle()

            for c in range(NC + 1):
                if c < NC:
                    gain(c)
                if 1 <= c <= NC:
                    variance(1, c - 1)
                if c < NC:
                    centre(1, c)
                if 1 <= c <= NC:
                    normalise(1, c - 1)
                if c == NC:
                    v.wait_ge(h_ready, NC)
                    link(nc.vector.tensor_scalar(rdeg[:, :], deg[:, :], 1.0, None, ALU.max))
                    link(nc.vector.tensor_scalar(has[:, :], deg[:, :], 1.0, None, ALU.min))
                    settle()
                    link(nc.vector.reciprocal(rdeg[:, :], rdeg[:, :]))
                    link(nc.vector.tensor_tensor(sq[:, :, :], b4b[:, :].unsqueeze(1).to_broadcast([NP, NT, D]),
                                                 bc(has[:, :], D), ALU.mult))
                    settle()
                    link(nc.vector.tensor_tensor(xs[:, :, :], xs[:, :, :], sq[:, :, :], ALU.add))
            v.wait_ge(hT_mm, NT // PW)
            link(nc.vector.memset(qsplit[:, :, :, 2 * H:RW].bitcast(F32), 0.0))
            link(nc.vector.memset(psplit[:, :, 2 * H:RW].bitcast(F32), 0.0))

            def step1(i, u):
                if i.valid(u, 1):
                    s = slot(u, 1)
                    wait_slot(v, hi1, i, u, 1, 2)
                    nc.vector.tensor_tensor(psplit[:, s % 2, H:2 * H], pwin[:, s % DEEP, :], psplit[:, s % 2, 0:H],
                                            ALU.subtract).then_inc(lo1[s % DEEP], 1)
                    nc.vector.tensor_tensor(qsplit[:, s % 2, :, H:2 * H], qrow[:, s, :, :],
                                            qsplit[:, s % 2, :, 0:H], ALU.subtract).then_inc(lo1[s % DEEP], 1)
                add_sums(1, P, [bank[6], bank[7]], i, u, 8)
                if i.valid(u, 0):
                    wait_slot(v, rel_in, i, u, 0, 16)
                    wait_slot(v, pre1, i, u, DEEP)
                    nc.vector.tensor_tensor(ST[:, u % DEEP, :], relb[:, u % DEEP, :],
                                            negid[:, 0:1].to_broadcast([P, GE]), ALU.is_equal)\
                        .then_inc(st_built[u % DEEP], 1)
                build_S(1, i, u, 4)
                if i.valid(u, 6):
                    s = slot(u, 6)
                    wait_slot(v, hi3, i, u, 6)
                    nc.vector.scalar_tensor_tensor(
                        h3[:, s % 2, :, H:2 * H], bank[4 + s % 2][:, 0:SUB * H].rearrange("p (k f) -> p k f", f=H),
                        0.0, h3[:, s % 2, :, 0:H], ALU.max, ALU.subtract).then_inc(lo3[s % DEEP], 1)

            v.wait_ge(acc_zero, 2)
            with v.Fori(0, nsweeps(v)) as s:
                sweep_start(1, s)
                run_steps(v, step1, 0, 8, s)
                sweep_end(1, s)
            v.sem_inc(done[1], 1)

            for m in range(NOUT):
                k = slice(m * OT, min((m + 1) * OT, NT))
                w = k.stop - k.start
                v.wait_ge(out_T, m + 1)
                link(nc.vector.tensor_tensor(tmp[:, k, :],
                                             bank[4 + m % 4][0:NP, 0:w * D].rearrange("p (t d) -> p t d", d=D),
                                             bc(rdeg[:, k], D), ALU.mult))
                settle()
                nc.vector.tensor_tensor(sq[:, k, :], tmp[:, k, :], xs[:, k, :], ALU.add).then_inc(fin, 1)

        @block.tensor
        def _(t):
            t.wait_ge(const, 3)
            t.wait_ge(dve, at["rmm"])
            for m in range(2):
                ins = nc.tensor.transpose(bank[m][0:NBLK, 0:P], rmm[:, m, :], ident[:, :])
            ins.then_inc(rmm_T, 1)
            for which, rows in (("srcT", src_r), ("dstT", dst_r)):
                t.wait_ge(dve, at["src_r"])
                for k in range(NTB):
                    nth = k + (NTB if which == "dstT" else 0)
                    if nth >= 6:
                        t.wait_ge(dve, at[("srcT", nth - 6)])
                    for b in range(k * per, min((k + 1) * per, NBLK)):
                        q = P if b < last else LASTQ
                        c = (b - k * per) * P
                        ins = nc.tensor.transpose(bank[2 + nth % 6][:, c:c + q], rows[0:q, b, :], ident[0:q, 0:q])
                    ins.then_inc(idx_T, 1)

            def step0(i, u):
                if not i.valid(u, 0):
                    return
                wait_slot(t, s_built[0], i, u, 0)
                wait_rows(t, gathered[0], i, u, 0)
                wait_slot(t, added[0], i, u, 2)
                for k in range(SUB):
                    for half in range(2):
                        ins = nc.tensor.matmul(bank[u % 2][0:WW, 0:WIN], wrow[:, u, k, half * D:half * D + WW],
                                               S[:, u % DEEP, k, :], start=(k == 0 and half == 0),
                                               stop=(k == SUB - 1 and half == 1))
                ins.then_inc(sums[0][u % DEEP], 1)

            t.wait_ge(dve, at["span"])
            with t.Fori(0, nsweeps(t)) as s:
                t.wait_ge(go[0], s + 1)
                run_steps(t, step0, 0, 0, s)
            t.wait_ge(done[0], 1)

            def aggregate(m):
                if m >= 2:
                    t.wait_ge(dve, at[("agg", m - 2)])
                for j in range(TC):
                    ins = nc.tensor.transpose(bank[m % 2][0:NP, j * (2 * D + 1):(j + 1) * (2 * D + 1)],
                                              accn[0:2 * D + 1, m * TC + j, :],
                                              ident[0:2 * D + 1, 0:2 * D + 1])
                ins.then_inc(agg_mm, 1)

            def turn(m):
                if m >= 2:
                    t.wait_ge(hT_ready, m - 1)
                nc.tensor.matmul(bank[2 + m % 2][:, 0:NPE],
                                 split[:, PW * m:PW * (m + 1), :, :].rearrange("p a b c -> p (a b c)"),
                                 identr[0:NP, 0:NPE], start=True, stop=True).then_inc(hT_mm, 1)

            def products(j):
                t.wait_ge(hT_ready, j + 1)
                b = j * PW // TC
                if b >= 4:
                    t.wait_ge(tab_ready, b - 3)
                w = PW * 2 * H
                k = j * PW % TC // PW * w
                for first, w_ in ((True, wpq_hi), (False, wpq_lo)):
                    ins = nc.tensor.matmul(bank[4 + b % 4][0:NP, k:k + w], hT[:, j % HTS, :],
                                           w_[:, :, :].rearrange("p a b -> p (a b)"),
                                           start=first, stop=not first)
                ins.then_inc(tab_mm, 1)

            ahead = CUTS[3] // TC
            for m in range(ahead):
                aggregate(m)
            t.wait_ge(weights, 1)
            for c in range(NC):
                t.wait_ge(h_ready, c + 1)
                rows = range(CUTS[c] // TC, CUTS[c + 1] // TC)
                more = range(ahead, CUTS[min(c + 4, NC)] // TC)
                ahead = more.stop
                for k in range(max(len(rows), len(more))):
                    if k < len(more):
                        aggregate(more[k])
                    if k < len(rows):
                        for m in range(rows[k] * TC // PW, (rows[k] + 1) * TC // PW):
                            turn(m)
                            if m >= 2:
                                products(m - 2)
            products(NT // PW - 2)
            products(NT // PW - 1)

            def step1(i, u):
                s1, s2, s3, s4 = (slot(u, lag) for lag in (1, 3, 5, 7))

                def own(half):
                    if i.valid(u, 1):
                        nc.tensor.matmul(bank[s1 % 2][0:H + 2, :], part(psplit[:, s1 % 2, :], half),
                                         ST[:, s1 % DEEP, :], start=(half == 0), stop=False)

                def neighbours(k):
                    if i.valid(u, 1):
                        for half in range(2):
                            ins = nc.tensor.matmul(bank[s1 % 2][0:H + 2, k * P:(k + 1) * P],
                                                   part(qsplit[:, s1 % 2, k, :], half), identr[:, :],
                                                   start=False, stop=(k == SUB - 1 and half == 1))
                        if k == SUB - 1:
                            ins.then_inc(pre1[s1 % DEEP], 1)

                def second():
                    if i.valid(u, 3):
                        wait_slot(t, act1, i, u, 3)
                        wait_slot(t, act2, i, u, 5)
                        nc.tensor.matmul(bank[2 + s2 % 2][:, :], w2s[:, :], h1[:, s2 % 2, :],
                                         start=True, stop=True).then_inc(pre2[s2 % DEEP], 1)

                def third(k):
                    if i.valid(u, 5):
                        ins = nc.tensor.matmul(bank[4 + s3 % 2][:, k * H:(k + 1) * H],
                                               h2[:, s3 % 2, k * P:(k + 1) * P], w3s[:, :],
                                               start=False, stop=(k == SUB - 1))
                        if k == SUB - 1:
                            ins.then_inc(pre3[s3 % DEEP], 1)

                def add_up(k):
                    if i.valid(u, 7):
                        ins = nc.tensor.matmul(bank[6 + s4 % 2][:, 0:WIN], h3[:, s4 % 2, k, :],
                                               S[:, s4 % DEEP, k, :], start=(k == 0), stop=(k == SUB - 1))
                        if k == SUB - 1:
                            ins.then_inc(sums[1][s4 % DEEP], 1)

                if i.valid(u, 5):
                    wait_slot(t, act2, i, u, 5)
                    wait_slot(t, lo3, i, u, 7)
                    nc.tensor.matmul(bank[4 + s3 % 2][:, 0:SUB * H], ones3[:, :],
                                     b3s[:, :, :].rearrange("p a b -> p (a b)"), start=True, stop=False)
                second()
                third(0)
                if i.valid(u, 1):
                    wait_slot(t, act1, i, u, 3)
                    wait_slot(t, st_built, i, u, 1)
                    wait_slot(t, lo1, i, u, 1, 2)
                own(0)
                third(1)
                own(1)
                third(2)
                neighbours(0)
                third(3)
                if i.valid(u, 7):
                    wait_slot(t, lo3, i, u, 7)
                    wait_slot(t, s_built[1], i, u, 7)
                    wait_slot(t, added[1], i, u, 9)
                add_up(0)
                neighbours(1)
                add_up(1)
                neighbours(2)
                add_up(2)
                neighbours(3)
                add_up(3)

            with t.Fori(0, nsweeps(t)) as s:
                t.wait_ge(go[1], s + 1)
                run_steps(t, step1, 0, 7, s)
            t.wait_ge(done[1], 1)

            def last_layer(m):
                if m >= 4:
                    t.wait_ge(out_copied, m - 3)
                w = len(range(m * OT, min((m + 1) * OT, NT), QUADS))
                for j in range(QUADS):
                    ins = nc.tensor.matmul(bank[m % 4][j * D:(j + 1) * D, 0:w * NP], w4s[:, :],
                                           accn[:, m * OT + j:min((m + 1) * OT, NT):QUADS, :],
                                           start=True, stop=True)
                ins.then_inc(out_mm, 1)

            def turn_back(m):
                t.wait_ge(out_copied, m + 1)
                if m >= 4:
                    t.wait_ge(fin, m - 3)
                for a in range(len(range(m * OT, min((m + 1) * OT, NT), QUADS))):
                    ins = nc.tensor.transpose(bank[4 + m % 4][0:NP, a * P:(a + 1) * P],
                                              h2[:, m % 2, a * NP:(a + 1) * NP], ident[:, :])
                ins.then_inc(out_T, 1)

            for m in range(NOUT + 1):
                if m < NOUT:
                    last_layer(m)
                if m >= 1:
                    turn_back(m - 1)

        @block.scalar
        def _(a):
            def square(l, c):
                a.wait_ge(centred, l * NC + c + 1)
                nc.scalar.activation(sq[:, chunk(c), :], tmp[:, chunk(c), :], ACT.Square).then_inc(squared, 1)

            def root(l, c):
                a.wait_ge(var_ready, l * NC + c + 1)
                nc.scalar.activation(std[:, chunk(c)], var[:, chunk(c)], ACT.Sqrt, bias=epsc[0:NP, :],
                                     scale=1.0 / D).then_inc(std_ready, 1)

            for k in range(P // D):
                a.dma_start(w1a[k * D:(k + 1) * D, :], W1[0:D, :]).then_inc(w_in, 16)
                a.dma_start(w1b[k * D:(k + 1) * D, :], W1[D:2 * D, :]).then_inc(w_in, 16)
            a.dma_start(w2s[:, :], W2).then_inc(w_in, 16)
            for k in range(2):
                a.dma_start(w4s[k * H:(k + 1) * H, :], W4).then_inc(w_in, 16)
            a.dma_start(b2c[:, :], b2.unsqueeze(1)).then_inc(w_in, 16)
            a.dma_start(w3s[:, :], W3).then_inc(w_in, 16)
            a.dma_start(b1c[:, :], b1.unsqueeze(1)).then_inc(w_in, 16)
            a.dma_start(brow[:, :], b3.unsqueeze(0).to_broadcast([3, H])).then_inc(w_in, 16)
            a.dma_start(b4b[:, :], b4.unsqueeze(0).to_broadcast([NP, D])).then_inc(w_in, 16)
            for k in range(NTB):
                a_, b_ = k * 512, min((k + 1) * 512, NSUB)
                a.wait_ge(idx_T, 1 + NTB + k)
                nc.scalar.activation(dstT[:, a_:b_], bank[2 + (NTB + k) % 6][:, 0:b_ - a_], ACT.Copy)\
                    .then_inc(dstT_ready, 1)
            for c in range(NC + 1):
                if c >= 1:
                    root(0, c - 1)
                if c < NC:
                    square(0, c)
                if c >= 1:
                    a.wait_ge(normed, c)
                    nc.scalar.activation(split[:, chunk(c - 1), 0, :], sq[:, chunk(c - 1), :], ACT.Copy)\
                        .then_inc(w_hi, 1)

            a.wait_ge(g_in, 16 * 6)
            for b in range(NBLK):
                q = P if b < last else LASTQ
                nc.scalar.activation(rel_r[0:q, b, :], dst_r[0:q, b, :], ACT.Identity,
                                     bias=base_row[0:q, b:b + 1], scale=-1.0).then_inc(rel_ready, 1)

            def copy_index(l, i, u):
                if i.valid(u, -LEAD):
                    k = slot(u, -LEAD)
                    wait_rows(a, gathered[l], i, u, RING - LEAD)
                    g = i.group + u + LEAD
                    nc.scalar.activation(idx[:, k, :], srcT[:, bass.ds(g * SUB, SUB)], ACT.Copy)\
                        .then_inc(idx_ready[l][k % DEEP], 1)

            def copies_done(l, s):
                for sm in idx_ready[l]:
                    a.wait_ge(sm, (s + 1) * (NG // DEEP))

            a.wait_ge(dve, at["span"])
            with a.Fori(0, nsweeps(a)) as s:
                a.wait_ge(go[0], s + 1)
                run_steps(a, lambda i, u: copy_index(0, i, u), LEAD, 0, s)
                copies_done(0, s)

            a.wait_ge(wtab_out, 16 * 2 * NC)

            def norm_step(c, q):
                if q == 0 and 1 <= c <= NC:
                    root(1, c - 1)
                if q == 1 and c < NC:
                    square(1, c)
                if q == 2 and 1 <= c <= NC:
                    k = chunk(c - 1)
                    a.wait_ge(normed, NC + c)
                    nc.scalar.activation(split[:, k, 0, :], sq[:, k, :], ACT.Copy).then_inc(h_hi, 1)

            def tables_out(c):
                def finish(b):
                    a.wait_ge(tab_mm, (b + 1) * TC // PW)
                    if c >= STAGES:
                        a.wait_ge(stage_out[c % STAGES], c // STAGES * 64)
                    k = b * TC - CUTS[c]
                    nc.scalar.activation(stage[:, c % STAGES, :, k:k + TC, :],
                                         bank[4 + b % 4][0:NP, :].rearrange("p (t c h) -> p c t h", t=TC, c=2),
                                         ACT.Copy).then_inc(tab_ready, 1)

                for b in range(CUTS[c] // TC, CUTS[c + 1] // TC):
                    for m in range(b * TC // PW, (b + 1) * TC // PW):
                        a.wait_ge(hT_mm, m + 1)
                        if m >= HTS:
                            a.wait_ge(tab_mm, m - HTS + 1)
                        nc.scalar.activation(hT[:, m % HTS, :], bank[2 + m % 2][:, 0:NP], ACT.Copy)\
                            .then_inc(hT_ready, 1)
                    if b > CUTS[c] // TC:
                        finish(b - 1)
                    norm_step(c + 2, b - CUTS[c] // TC)
                for q in range((CUTS[c + 1] - CUTS[c]) // TC, 3):
                    norm_step(c + 2, q)
                finish(CUTS[c + 1] // TC - 1)

            a.wait_ge(rel_out, 32)
            for c in range(2):
                for q in range(3):
                    norm_step(c, q)
            for c in range(NC):
                tables_out(c)

            def step1(i, u):
                copy_index(1, i, u)
                if i.valid(u, 0):
                    wait_slot(a, pre1, i, u, 2)
                    wait_slot(a, pwin_in, i, u, 0, 16)
                    nc.scalar.activation(psplit[:, u % 2, 0:H], pwin[:, u % DEEP, :], ACT.Copy)\
                        .then_inc(hi1[u % DEEP], 1)
                    wait_rows(a, gathered[1], i, u, 0)
                    nc.scalar.activation(qsplit[:, u % 2, :, 0:H], qrow[:, u, :, :], ACT.Copy)\
                        .then_inc(hi1[u % DEEP], 1)
                if i.valid(u, 2):
                    s = slot(u, 2)
                    wait_slot(a, pre1, i, u, 2)
                    wait_slot(a, pre2, i, u, 4)
                    nc.scalar.activation(h1[:, s % 2, :], bank[s % 2][0:H, :], ACT.Relu, bias=b1c[:, 0:1])\
                        .then_inc(act1[s % DEEP], 1)
                if i.valid(u, 4):
                    s = slot(u, 4)
                    wait_slot(a, pre2, i, u, 4)
                    wait_slot(a, pre3, i, u, 6)
                    nc.scalar.activation(h2[:, s % 2, :], bank[2 + s % 2][:, :], ACT.Relu, bias=b2c[:, 0:1])\
                        .then_inc(act2[s % DEEP], 1)
                if i.valid(u, 6):
                    s = slot(u, 6)
                    wait_slot(a, pre3, i, u, 6)
                    wait_slot(a, sums[1], i, u, 8)
                    nc.scalar.activation(h3[:, s % 2, :, 0:H],
                                         bank[4 + s % 2][:, 0:SUB * H].rearrange("p (k f) -> p k f", f=H),
                                         ACT.Relu).then_inc(hi3[s % DEEP], 1)

            with a.Fori(0, nsweeps(a)) as s:
                a.wait_ge(go[1], s + 1)
                run_steps(a, step1, LEAD, 6, s)
                copies_done(1, s)

            for m in range(NOUT):
                w = len(range(m * OT, min((m + 1) * OT, NT), QUADS)) * NP
                a.wait_ge(out_mm, m + 1)
                if m >= 2:
                    a.wait_ge(out_T, m - 1)
                nc.scalar.activation(h2[:, m % 2, 0:w], bank[m % 4][:, 0:w], ACT.Copy).then_inc(out_copied, 1)

        @block.gpsimd
        def _(g):
            n = [0]

            def link(ins):
                n[0] += 1
                ins.then_inc(pool, 1)

            def settle():
                g.wait_ge(pool, n[0])

            nc.gpsimd.iota(iota_i[:, :], pattern=[[1, P]], base=0, channel_multiplier=0).then_inc(const, 1)
            nc.gpsimd.iota(negid_i[:, :], pattern=[[0, 1]], base=0, channel_multiplier=-1).then_inc(const, 1)
            link(nc.gpsimd.memset(ident[:, :], 0.0))
            settle()
            link(nc.gpsimd.affine_select(out=ident[:, :], in_=ident[:, :], compare_op=ALU.not_equal, fill=1.0,
                                         base=0, pattern=[[-1, P]], channel_multiplier=1))
            settle()
            nc.gpsimd.tensor_copy(identr[:, :], ident[:, :]).then_inc(const, 1)
            link(nc.gpsimd.memset(wrow[:, :, :, 2 * D + 1:D + WW].bitcast(F32), 0.0))
            link(nc.gpsimd.memset(wrow[:, :, :, 2 * D:2 * D + 1].bitcast(F32), 1.0))
            settle()
            link(nc.gpsimd.memset(wpq[:, :, :], 0.0))
            settle()
            nc.gpsimd.memset(acc[0:2 * D + 1, :], 0.0).then_inc(acc_zero, 1)
            g.wait_ge(w_in, 16 * 16)
            g.wait_ge(acc_zero, 1)
            for k in range(P // D):
                r = slice(k * D, (k + 1) * D)
                link(nc.gpsimd.tensor_tensor(wpq[r, k // 2, 0:H], w1a[r, :], w1b[r, :], ALU.subtract))
                settle()
                link(nc.gpsimd.tensor_copy(wpq[r, k // 2, H:2 * H], w1b[r, :]))
                settle()
            link(nc.gpsimd.tensor_copy(wpq_hi[:, :, :], wpq[:, :, :]))
            settle()
            link(nc.gpsimd.tensor_tensor(wpq_lo[:, :, :], wpq[:, :, :], wpq_hi[:, :, :], ALU.subtract))
            settle()
            for k in range(3):
                link(nc.gpsimd.tensor_copy(bpart[:, k, :], brow[:, :]))
                settle()
                if k < 2:
                    link(nc.gpsimd.tensor_tensor(brow[:, :], brow[:, :], bpart[:, k, :], ALU.subtract))
                    settle()
            link(nc.gpsimd.tensor_tensor(bmask[:, :, :], bpart[:, :, :], bc(ident[0:3, 0:3], H), ALU.mult))
            settle()
            for k in range(1, 3):
                link(nc.gpsimd.tensor_tensor(bmask[:, 0, :], bmask[:, 0, :], bmask[:, k, :], ALU.add))
                settle()
            nc.gpsimd.tensor_copy(b3s[:, :, :], bmask[:, 0:1, :].to_broadcast([3, SUB, H])).then_inc(weights, 1)

            for c in range(NC):
                k = chunk(c)
                g.wait_ge(w_hi, c + 1)
                if c == 0:
                    g.wait_ge(weights, 1)
                else:
                    g.wait_ge(w_lo, c)
                nc.gpsimd.tensor_tensor(split[:, k, 1, :], sq[:, k, :], split[:, k, 0, :], ALU.subtract)\
                    .then_inc(w_lo, 1)

            def gathers(l, table, rows, stored, total):
                def step(i, u):
                    wait_slot(g, idx_ready[l], i, u, 0)
                    wait_slot(g, sums[0] if l == 0 else lo1, i, u, RING, 1 + l)
                    g.sem_inc(opened[l], 1)
                    g.wait_ge(stored, total)
                    for k in range(real_subtiles(i, u)):
                        nc.gpsimd.indirect_dma_start(
                            out=rows[:, u, k, :], out_offset=None, in_=table,
                            in_offset=bass.IndirectOffsetOnAxis(ap=idx[:, u, k:k + 1], axis=0))\
                            .then_inc(gathered[l][u], 16)
                return step

            g.wait_ge(dve, at["span"])
            with g.Fori(0, nsweeps(g)) as s:
                g.wait_ge(go[0], s + 1)
                run_steps(g, gathers(0, wtab, wrow[:, :, :, 0:2 * D].bitcast(F32), wtab_out, 16 * 2 * NC), 0, 0, s)

            accs = acc[:, 0:N].rearrange("f (p t) -> f p t", t=NT)
            g.wait_ge(done[0], 1)
            link(nc.gpsimd.memset(acc[:, N:N + WIN], 0.0))
            settle()
            for c in range(NC):
                k = chunk(c)
                g.wait_ge(h_hi, c + 1)
                nc.gpsimd.tensor_tensor(split[:, k, 1, :], sq[:, k, :], split[:, k, 0, :], ALU.subtract)\
                    .then_inc(h_ready, 1)
                g.wait_ge(h_ready, c + 1)
                g.wait_ge(agg_mm, CUTS[c + 1] // TC)
                link(nc.gpsimd.memset(accs[:, :, k], 0.0))
                settle()
            g.sem_inc(acc_zero, 1)
            for r, sm in enumerate(stage_out):
                g.wait_ge(sm, stored(r))
            with g.Fori(0, nsweeps(g)) as s:
                g.wait_ge(go[1], s + 1)
                run_steps(g, gathers(1, qtab, qrow, stage_out[0], stored(0)), 0, 0, s)

        @block.sync
        def _(y):
            full = last * P * P
            mid = full + REALQ * P
            for ids, tile_, landed in ((dst, dst_i, dst_in), (src, src_i, src_in)):
                y.dma_start(tile_[:, 0:last, :], ids[0:full].rearrange("(b q e) -> q b e", q=P, e=P))\
                    .then_inc(landed, 16)
                y.dma_start(tile_[0:REALQ, last, :], ids[full:mid].rearrange("(q e) -> q e", e=P))\
                    .then_inc(landed, 16)
                y.dma_start(tile_[REALQ:REALQ + 1, last, 0:REALR], ids[mid:E].unsqueeze(0)).then_inc(landed, 16)
                y.dma_start(tile_[REALQ:REALQ + 1, last, REALR:P], ids[E - (P - REALR):E].unsqueeze(0))\
                    .then_inc(landed, 16)
                k = LASTQ - REALQ - 1
                y.dma_start(tile_[REALQ + 1:LASTQ, last, :],
                            ids[E - k * P:E].rearrange("(q e) -> q e", e=P)).then_inc(landed, 16)
            for a, b in PARTS:
                y.dma_start(xs[a:b, :, :], xd[a:b, :, :]).then_inc(x_in, 16)
                y.dma_start(n1[a:b, :], nv1.rearrange("(p t) o -> p (t o)", t=NT)[a:b, :]).then_inc(x_in, 16)
                y.dma_start(n2[a:b, :], nv2.rearrange("(p t) o -> p (t o)", t=NT)[a:b, :]).then_inc(x_in, 16)
            y.wait_ge(dve, at["gmm"])
            y.dma_start(gmin_d.rearrange("(b g) -> b g", g=GB), gmm[:, 0, :]).then_inc(g_out, 16)
            y.dma_start(gmax_d.rearrange("(b g) -> b g", g=GB), gmm[:, 1, :]).then_inc(g_out, 16)
            y.wait_ge(g_out, 32)
            y.dma_start(base0[:, :], gmin_d[0:NG].unsqueeze(0).to_broadcast([P, NG])).then_inc(g_in, 16)
            y.dma_start(gtop[:, :], gmax_d[0:NG].unsqueeze(0).to_broadcast([P, NG])).then_inc(g_in, 16)
            for r in range(SUB):
                y.dma_start(base_row[r:P:SUB, :], gmin_d.rearrange("(b g) -> g b", g=GB),
                            allow_slow_non_contiguous=True).then_inc(g_in, 16)
            wd = wtab.rearrange("(p t) (c d) -> p t c d", t=NT, c=2)
            for c in range(NC):
                y.wait_ge(w_lo, c + 1)
                for a, b in PARTS:
                    y.dma_start(wd[a:b, chunk(c), :, :], split[a:b, chunk(c), :, :].bitcast(F32)).then_inc(wtab_out, 16)
            y.dma_start(ptab[N:N + WIN, :], zrow[:, :]).then_inc(z_out, 16)
            y.wait_ge(rel_ready, NBLK)
            y.dma_start(rel_d[0:last * P, :].rearrange("(b q) e -> q b e", q=P), rel_r[:, 0:last, :])\
                .then_inc(rel_out, 16)
            y.dma_start(rel_d[last * P:NSUB, :], rel_r[0:LASTQ, last, :]).then_inc(rel_out, 16)
            tables = [tab.rearrange("(p t) h -> p t h", t=NT) for tab in (ptab[0:N, :], qtab)]
            for c in range(NC):
                y.wait_ge(tab_ready, CUTS[c + 1] // TC)
                for a, b in PARTS:
                    for k, table in enumerate(tables):
                        y.dma_start(table[a:b, chunk(c), :], stage[a:b, c % STAGES, k, 0:CUTS[c + 1] - CUTS[c], :])\
                            .then_inc(stage_out[c % STAGES], 16)
            y.wait_ge(z_out, 16)
            y.wait_ge(rel_out, 32)
            for r, sm in enumerate(stage_out):
                y.wait_ge(sm, stored(r))

            relg = rel_d.rearrange("(g k) e -> g (k e)", k=SUB)

            def step1(i, u):
                g = i.group + u
                wait_slot(y, st_built, i, u, DEEP)
                y.dma_start(relb[:, u % DEEP, :], relg[bass.ds(g, 1), :].to_broadcast([P, GE]))\
                    .then_inc(rel_in[u % DEEP], 16)
                base = y.value_load(base_i[0:1, bass.ds(g, 1)], min_val=0, max_val=N)
                wait_slot(y, lo1, i, u, DEEP, 2)
                y.dma_start(pwin[:, u % DEEP, :], ptab[bass.ds(base, WIN), :]).then_inc(pwin_in[u % DEEP], 16)

            with y.Fori(0, nsweeps(y)) as s:
                y.wait_ge(go[1], s + 1)
                run_steps(y, step1, 0, 0, s)

            ends = [0, 4, 6, NOUT]
            for m0, m1 in zip(ends, ends[1:]):
                y.wait_ge(fin, m1)
                k = slice(m0 * OT, min(m1 * OT, NT))
                for a, b in PARTS:
                    y.dma_start(od[a:b, k, :], sq[a:b, k, :]).then_inc(out_s, 16)
            y.wait_ge(out_s, 16 * 2 * (len(ends) - 1))


_INS = ["x", "src", "dst", "node_vec1", "node_vec1_n2", "L1_gnn_W1", "L1_gnn_b1", "L1_gnn_W2", "L1_gnn_b2",
        "L1_gnn_W3", "L1_gnn_b3", "L1_gnn_W4", "L1_gnn_b4"]


def kernel(**inputs):
    import numpy as _np
    import concourse.bacc as _bacc
    from concourse import mybir as _mybir
    from concourse.bass_utils import run_bass_kernel_spmd as _run

    nc = _bacc.Bacc("TRN2", target_bir_lowering=False, num_devices=1)
    arrays, args = {}, []
    for name in _INS:
        a = _np.ascontiguousarray(inputs[name])
        arrays[f"in_{name}_dram"] = a
        args.append(nc.dram_tensor(f"in_{name}_dram", a.shape, _mybir.dt.from_np(a.dtype), kind="ExternalInput").ap())
    args.append(nc.dram_tensor("out_dram", (N, D), _mybir.dt.float32, kind="ExternalOutput").ap())
    build(nc, *args)
    r = _run(nc, [arrays], core_ids=[0])
    return r.results[0]["out_dram"]
```
